# Optimizing a Trainium2 kernel written in Bass

```python
import numpy as np
import jax
import jax.numpy as jnp

def _softmax(x, axis=-1):
    return jax.nn.softmax(x, axis=axis)

def _gelu(x):
    return jax.nn.gelu(x, approximate=True)

def _silu(x):
    return jax.nn.silu(x)

def _sigmoid(x):
    return jax.nn.sigmoid(x)

def _layernorm(x, axis=-1, eps=1e-05):
    m = jnp.mean(x, axis=axis, keepdims=True)
    v = jnp.var(x, axis=axis, keepdims=True)
    return (x - m) / jnp.sqrt(v + eps)

def _scatter_add(tgt, idx, src, axis=0):
    return tgt.at[idx].add(src)

def _segment_sum(src, seg, n):
    return jax.ops.segment_sum(src, seg, n)
kernel_name = 'mk_sandwich_d1_jaxref_r8_d1a82f'

def setup_inputs(seed: int=0):
    np.random.seed(seed)
    _w = jnp.asarray

    def _L0_attn_setup():
        import jax, jax.numpy as jnp
        import numpy as np
        D_MODEL = 128
        N_HEADS = 16
        HEAD_DIM = D_MODEL // N_HEADS
        SCALE = HEAD_DIM ** (-0.5)
        MIN_VAL = jnp.finfo(jnp.float32).min

        def _split_heads(y):
            B, T, _ = y.shape
            return y.reshape(B, T, N_HEADS, HEAD_DIM).transpose(0, 2, 1, 3)
        key = jax.random.key(seed)
        ks = jax.random.split(key, 7)
        B, T = (1, 256)
        s = D_MODEL ** (-0.5)
        return {'x': jax.random.normal(ks[0], (B, T, D_MODEL), dtype=jnp.float32), 'Wq': jax.random.normal(ks[1], (D_MODEL, D_MODEL), dtype=jnp.float32) * s, 'Wk1': jax.random.normal(ks[2], (D_MODEL, D_MODEL), dtype=jnp.float32) * s, 'Wk2': jax.random.normal(ks[3], (D_MODEL, D_MODEL), dtype=jnp.float32) * s, 'Wv': jax.random.normal(ks[4], (D_MODEL, D_MODEL), dtype=jnp.float32) * s, 'Wo': jax.random.normal(ks[5], (D_MODEL, D_MODEL), dtype=jnp.float32) * s, 'lambda_logit': jnp.zeros((N_HEADS,), dtype=jnp.float32)}
    _L0_attn_in = _L0_attn_setup()

    def _L0_ffn_setup():
        import jax, jax.numpy as jnp
        import numpy as np
        DIM = 128
        HIDDEN = 512
        E = 8
        K = 2

        def _ffn_hidden(h, multiple_of=32):
            h = int(2 * h / 3)
            return multiple_of * ((h + multiple_of - 1) // multiple_of)
        EXP_HID = _ffn_hidden(HIDDEN)
        SH_HID = _ffn_hidden(HIDDEN // 2)

        def _swiglu(t, a, b, c):
            return jax.nn.silu(t @ a) * (t @ c) @ b
        key = jax.random.key(seed)
        ks = jax.random.split(key, 8)

        def xavier(k, shape, fan_in, fan_out):
            lim = np.sqrt(6.0 / (fan_in + fan_out)).astype(np.float32)
            return jax.random.uniform(k, shape, jnp.float32, -lim, lim)
        return {'x': jax.random.normal(ks[0], (2, 256, DIM), jnp.float32), 'gate_w': xavier(ks[1], (E, DIM), DIM, E), 'w1': xavier(ks[2], (E, DIM, EXP_HID), DIM, EXP_HID), 'w2': xavier(ks[3], (E, EXP_HID, DIM), EXP_HID, DIM), 'w3': xavier(ks[4], (E, DIM, EXP_HID), DIM, EXP_HID), 'sw1': xavier(ks[5], (DIM, SH_HID), DIM, SH_HID), 'sw2': xavier(ks[6], (SH_HID, DIM), SH_HID, DIM), 'sw3': xavier(ks[7], (DIM, SH_HID), DIM, SH_HID)}
    _L0_ffn_in = _L0_ffn_setup()
    _d = {'L0_attn_x': _L0_attn_in['x'], 'L0_attn_Wq': _L0_attn_in['Wq'], 'L0_attn_Wk1': _L0_attn_in['Wk1'], 'L0_attn_Wk2': _L0_attn_in['Wk2'], 'L0_attn_Wv': _L0_attn_in['Wv'], 'L0_attn_Wo': _L0_attn_in['Wo'], 'L0_attn_lambda_logit': _L0_attn_in['lambda_logit'], 'L0_ffn_gate_w': _L0_ffn_in['gate_w'], 'L0_ffn_w1': _L0_ffn_in['w1'], 'L0_ffn_w2': _L0_ffn_in['w2'], 'L0_ffn_w3': _L0_ffn_in['w3'], 'L0_ffn_sw1': _L0_ffn_in['sw1'], 'L0_ffn_sw2': _L0_ffn_in['sw2'], 'L0_ffn_sw3': _L0_ffn_in['sw3']}
    _x0 = _d['L0_attn_x']
    _d['L0_attn_x'] = jax.random.normal(jax.random.fold_in(jax.random.key(seed), 1), (8, 512, 128), dtype=_x0.dtype)
    del _x0
    return _d

def reference(L0_attn_x, L0_attn_Wq, L0_attn_Wk1, L0_attn_Wk2, L0_attn_Wv, L0_attn_Wo, L0_attn_lambda_logit, L0_ffn_gate_w, L0_ffn_w1, L0_ffn_w2, L0_ffn_w3, L0_ffn_sw1, L0_ffn_sw2, L0_ffn_sw3):

    def _L0_attn_ref(x, Wq, Wk1, Wk2, Wv, Wo, lambda_logit):
        import jax, jax.numpy as jnp
        import numpy as np
        D_MODEL = 128
        N_HEADS = 16
        HEAD_DIM = D_MODEL // N_HEADS
        SCALE = HEAD_DIM ** (-0.5)
        MIN_VAL = jnp.finfo(jnp.float32).min

        def _split_heads(y):
            B, T, _ = y.shape
            return y.reshape(B, T, N_HEADS, HEAD_DIM).transpose(0, 2, 1, 3)
        B, T, _ = x.shape
        q = _split_heads(x @ Wq.T)
        k1 = _split_heads(x @ Wk1.T)
        k2 = _split_heads(x @ Wk2.T)
        v = _split_heads(x @ Wv.T)
        s1 = jnp.einsum('bhqd,bhkd->bhqk', q, k1) * SCALE
        s2 = jnp.einsum('bhqd,bhkd->bhqk', q, k2) * SCALE
        causal = jnp.arange(T)[None, :] <= jnp.arange(T)[:, None]
        s1 = jnp.where(causal[None, None], s1, MIN_VAL)
        s2 = jnp.where(causal[None, None], s2, MIN_VAL)
        attn_exp = jax.nn.softmax(s1, axis=-1)
        attn_noise = jax.nn.softmax(s2, axis=-1)
        lam = jax.nn.sigmoid(lambda_logit)[None, :, None, None]
        attn = attn_exp - lam * attn_noise
        denom = jnp.maximum(jnp.sum(jnp.abs(attn), axis=-1, keepdims=True), 1e-06)
        attn = attn / denom
        out = jnp.einsum('bhqk,bhkd->bhqd', attn, v)
        out = out.transpose(0, 2, 1, 3).reshape(B, T, D_MODEL)
        return out @ Wo.T

    def _L0_ffn_ref(x, gate_w, w1, w2, w3, sw1, sw2, sw3):
        import jax, jax.numpy as jnp
        import numpy as np
        DIM = 128
        HIDDEN = 512
        E = 8
        K = 2

        def _ffn_hidden(h, multiple_of=32):
            h = int(2 * h / 3)
            return multiple_of * ((h + multiple_of - 1) // multiple_of)
        EXP_HID = _ffn_hidden(HIDDEN)
        SH_HID = _ffn_hidden(HIDDEN // 2)

        def _swiglu(t, a, b, c):
            return jax.nn.silu(t @ a) * (t @ c) @ b
        B, S, D = x.shape
        xt = x.reshape(-1, D)
        T = xt.shape[0]
        logits = xt @ gate_w.T
        scores = jax.nn.softmax(logits, axis=-1)
        topk_w, topk_i = jax.lax.top_k(scores, K)
        comb = jnp.zeros((T, E), x.dtype).at[jnp.arange(T)[:, None], topk_i].add(topk_w)
        y = jnp.zeros_like(xt)
        for e in range(E):
            y = y + comb[:, e:e + 1] * _swiglu(xt, w1[e], w2[e], w3[e])
        y = y.reshape(B, S, D)
        return y + _swiglu(x, sw1, sw2, sw3)
    x = L0_attn_x
    x = x + _layernorm(_L0_attn_ref(_layernorm(x, axis=-1), L0_attn_Wq, L0_attn_Wk1, L0_attn_Wk2, L0_attn_Wv, L0_attn_Wo, L0_attn_lambda_logit), axis=-1)
    x = x + _layernorm(_L0_ffn_ref(_layernorm(x, axis=-1), L0_ffn_gate_w, L0_ffn_w1, L0_ffn_w2, L0_ffn_w3, L0_ffn_sw1, L0_ffn_sw2, L0_ffn_sw3), axis=-1)
    return x

_drawn_inputs = setup_inputs


def setup_inputs(seed=0):
    import zlib

    import numpy as np

    out = dict(_drawn_inputs(seed))
    spreads = {'L0_attn_lambda_logit': (0.0, 0.1)}
    factors = {}
    for name, (base, spread) in spreads.items():
        noise = np.random.default_rng([zlib.crc32(name.encode()), seed]).standard_normal(out[name].shape)
        drawn = base * np.exp(spread * noise) if base else spread * noise
        out[name] = jnp.asarray(drawn.astype(out[name].dtype))
    for name, factor in factors.items():
        out[name] = (out[name] * factor).astype(out[name].dtype)
    return out
```

```python
import concourse.bass as bass
from concourse import mybir
from contextlib import ExitStack


def diff_attention_moe_layer(nc, x, Wq, Wk1, Wk2, Wv, Wo, lam, gate_w, w1, w2, w3, sw1, sw2, sw3, out):
    fp32, bf16 = mybir.dt.float32, mybir.dt.bfloat16
    ALU, ACT, AX = mybir.AluOpType, mybir.ActivationFunctionType, mybir.AxisListType

    B, T, D = x.shape
    P = 128
    H = lam.shape[0]
    HD = D // H
    NJ = T // P
    G = 4
    NG = H // G
    STEPS = NJ * NG
    SLOTS = STEPS * G
    E, _, HID = w1.shape
    SH = sw1.shape[1]
    SCALE = float(HD) ** -0.5
    EPS = 1e-5
    PARTS = 3
    KR = PARTS * PARTS * HD
    RING = 3

    groups = [[(0, P), (P, SH - P)]] + [[(0, P), (P, P), (2 * P, HID - 2 * P)] for _ in range(E)]
    items = [(e, c, rows) for e, ch in enumerate(groups) for c, (_, rows) in enumerate(ch)]
    NI = len(items)
    last_item = {e: k for k, (e, _, _) in enumerate(items)}
    NE = len(groups)
    FIRST_SLOT, LAST_SLOT = 18, 56
    weight = lambda s: s // (G * NG) + 1
    span = sum(weight(s) for s in range(FIRST_SLOT, LAST_SLOT))
    item_at, acc = {}, 0
    for s in range(FIRST_SLOT, LAST_SLOT + 1):
        k = len(item_at)
        if k < NI and acc * (NI - 1) >= k * span:
            item_at[s] = k
        acc += weight(s)
    assert len(item_at) == NI
    slot_of = {k: s for s, k in item_at.items()}
    gate_at = {slot_of[k] + 1: k for k in range(NI)}
    down_at = {slot_of[last_item[e]] + 2: e for e in range(NE)}
    comb_at = {slot_of[last_item[e]] + 3: e for e in range(NE)}
    FINAL_STATS, FINAL_APPLY = 61, 63
    assert max(comb_at) < FINAL_STATS

    scratch = nc.dram_tensor("qk_parts", (3, PARTS, HD, H, T), bf16).ap()

    ctx = ExitStack()
    with ctx:
        def sb(name, shape, dt=fp32):
            return ctx.enter_context(nc.sbuf_tensor(name, shape, dt))

        def bank(name):
            return ctx.enter_context(nc.psum_tensor(name, [P, 512], fp32))

        def sem(name):
            return ctx.enter_context(nc.semaphore(name))

        stacks = [sb(n, [KR, H, T], bf16) for n in ("q_stack", "k1_stack", "k2_stack")]
        ex = sb("ex", [P, 2, 2, G, T])
        xT = sb("xT", [P, G, T])
        vpad = sb("vpad", [P, NJ, H, 32])
        w1s, w3s = sb("w1s", [P, NI, P]), sb("w3s", [P, NI, P])
        w2s = sb("w2s", [P, NI, P])
        gact = sb("gact", [P, 2, 3, T])
        th, prod = sb("th", [P, 2, T]), sb("prod", [P, 2, T])
        n2T_new, n2T = sb("n2T_new", [P, T]), sb("n2T", [P, T])
        x1_new, x1 = sb("x1_new", [P, NJ, D]), sb("x1", [P, NJ, D])
        yacc, yexp = sb("yacc", [P, NJ, D]), sb("yexp", [P, 2, NJ, D])
        xin, n1T, xres = sb("xin", [P, NJ, D]), sb("n1T", [P, T]), sb("xres", [P, NJ, D])
        qf = sb("qf", [P, 3, T])
        parts = sb("parts", [P, 3, PARTS, T], bf16)
        osb = sb("osb", [P, NG, P])
        on, onT, ao, n2 = sb("on", [P, H, HD]), sb("onT", [P, P]), sb("ao", [P, D]), sb("n2", [P, D])
        wT = sb("wT", [P, 5, P])
        gT = sb("gT", [P, E])
        ident = sb("ident", [P, P])
        identb, maskb = sb("identb", [P, P], bf16), sb("maskb", [P, P], bf16)
        maskf = sb("maskf", [P, P])
        nlam = sb("nlam", [P, H])
        nm = sb("nm", [P, 2, G, 2])
        Z = sb("Z", [P, 2, 2, G])
        rz, cz, nc_ = sb("rz", [P, G]), sb("cz", [P, G]), sb("negc", [P, G])
        zg, den, rden, sab = sb("zg", [P, G]), sb("den", [P, H]), sb("rden", [P, H]), sb("sab", [P, G])
        half = sb("half", [P, 4])
        kinds = ("in", "att", "x1", "out")
        bst = {k: sb(f"bst_{k}", [P, NJ, 6]) for k in kinds}
        mv = {k: sb(f"mv_{k}", [P, NJ, 2]) for k in kinds}
        ve = {k: sb(f"ve_{k}", [P, NJ]) for k in kinds}
        rstd = {k: sb(f"rstd_{k}", [P, NJ]) for k in kinds}
        lg, sc, se = sb("lg", [P, NJ, E]), sb("sc", [P, NJ, E]), sb("se", [P, NJ])
        m8, lmx = sb("m8", [P, NJ, 8]), sb("lmx", [P, NJ])
        gtv, eqv, cum, comb = sb("gtv", [P, NJ, E]), sb("eqv", [P, NJ, E]), sb("cum", [P, NJ, E]), sb("comb", [P, NJ, E])
        cgt, keep = sb("cgt", [P, NJ]), sb("keep", [P, NJ, E])
        fence_cell, xres_cell = sb("fence_cell", [P, 1]), sb("xres_cell", [P, 1])
        wload = xT[:, 0:2, :].rearrange("p a b -> p (a b)")

        S = [bank(f"S{i}") for i in range(RING)]
        TB, OB, H1B, H3B, YB = bank("TB"), bank("OB"), bank("H1B"), bank("H3B"), bank("YB")

        names = """
        ld_w ld_ffn ld_x ld_xres ld_lam pool_consts lam_exp
        s_full s_free nm_ready last_exps x_ready e_free t_full t_evac t1_full
        o_full o_evac on_ready y_full h1_full h3_full h1c_ready acc_done n2t_ready n2_ready
        st_in st_att st_x1 st_out rs_in rs_att rs_x1 rs_out n1_ready xin_free xres_free
        parts_ready parts_stored parts_free stack_in_use stack_free logits_ready gexp_ready
        out_ready out_stored dve_chain pool_chain pe_setup
        qf_mono p_mono y_mono g_mono""".split()
        q = {n: sem(n) for n in names}
        stack_loaded = [sem(f"stack_loaded{g}") for g in range(NG)]
        q.update({f"stack_loaded{g}": s for g, s in enumerate(stack_loaded)})

        class Tally:

            def __init__(self, eng, rings=()):
                self.eng, self.n = eng, {}
                for name, depth in rings:
                    self.n[name] = -depth

            def next(self, name, k=1):
                self.n[name] = self.n.get(name, 0) + k
                return self.n[name]

            def wait(self, name, k=1):
                v = self.next(name, k)
                if v > 0:
                    self.eng.wait_ge(q[name], v)

            def rebase(self):
                for name, v in self.n.items():
                    if v > 0:
                        self.eng.wait_ge(q[name], v)
                        self.eng.sem_inc(q[name], -v)
                    self.n[name] = min(v, 0)

        def p_base(b):
            return NI * (b - 1)

        Y_BODY = NE + 2 * NJ

        def y_base(b):
            return 0 if isinstance(b, int) and b == 0 else b * Y_BODY - (NE + 2)

        block = ctx.enter_context(nc.Block())

        def bodies(eng, f):
            f(0, True, False, True)
            with eng.Fori(1, B - 1) as b:
                f(b, True, True, True)
            f(B - 1, True, True, False)
            f(B, False, True, False)

        def fills(n):
            return [[0, 1]] if n // NG <= 1 else [[0], [1]]

        FILLS = sum(G * len(fills(n)) for n in range(STEPS))
        assert FILLS % RING == 0
        first_fill = [sum(G * len(fills(m)) for m in range(n)) for n in range(STEPS)]

        @block.sync
        def _(sp):
            t = Tally(sp)

            def store_parts_and_stack(wait_free):
                for m in range(3):
                    t.wait("parts_ready")
                    for i in range(PARTS):
                        sp.dma_start(scratch[m, i].rearrange("d h t -> h d t"),
                                     parts[:, m, i, :]).then_inc(q["parts_stored"], 16)
                t.wait("parts_stored", 16 * 3 * PARTS)
                sp.sem_inc(q["parts_free"], 1)
                for g in range(NG):
                    if wait_free:
                        t.wait("stack_free")
                    hs = slice(G * g, G * (g + 1))
                    for i in range(PARTS):
                        for jj in range(PARTS):
                            r = (PARTS * i + jj) * HD
                            sp.dma_start(stacks[0][r:r + HD, hs, :],
                                         scratch[0, i, :, hs, :]).then_inc(stack_loaded[g], 16)
                        r = PARTS * i * HD
                        for m in (1, 2):
                            sp.dma_start(stacks[m][r:r + PARTS * HD, hs, :],
                                         scratch[m, :, :, hs, :].rearrange("i d h t -> (i d) h t")
                                         ).then_inc(stack_loaded[g], 16)

            def load_rows(dst, b):
                return sp.dma_start(dst[:, :, :], x[b].rearrange("(j p) d -> p j d", p=P)
                                    if isinstance(b, int) else
                                    x[bass.ds(b, 1)].rearrange("a (j p) d -> (a p) j d", p=P))

            load_rows(xin, 0).then_inc(q["ld_x"], 16)
            for i, w in enumerate((Wq, Wk1, Wk2, Wv, Wo)):
                sp.dma_start(wload[:, i * P:(i + 1) * P], w).then_inc(q["ld_w"], 16)
            sp.dma_start(wload[0:E, 5 * P:6 * P], gate_w).then_inc(q["ld_w"], 16)
            load_rows(xres, 0).then_inc(q["ld_xres"], 16)
            store_parts_and_stack(False)

            def body(b, attn, prev, nxt):
                if nxt:
                    t.wait("xin_free")
                    load_rows(xin, b + 1).then_inc(q["ld_x"], 16)
                if prev and attn:
                    t.wait("xres_free")
                    load_rows(xres, b).then_inc(q["ld_xres"], 16)
                if nxt:
                    t.wait("stack_in_use")
                    store_parts_and_stack(True)
                if prev:
                    t.wait("out_ready")
                    o = out[b - 1].rearrange("(j p) d -> p j d", p=P) if isinstance(b, int) else \
                        out[bass.ds(b - 1, 1)].rearrange("a (j p) d -> (a p) j d", p=P)
                    sp.dma_start(o, yacc[:, :, :]).then_inc(q["out_stored"], 16)
                t.rebase()

            t.rebase()
            bodies(sp, body)

        @block.gpsimd
        def _(pool):
            t = Tally(pool)
            gp = nc.gpsimd
            pool.sem_inc(q["out_stored"], 16)

            def chain(ins):
                ins.then_inc(q["pool_chain"], 1)
                t.wait("pool_chain")

            def wait_mono(name, value):
                pool.wait_ge(q[name], value)
                pool.sem_inc(q["pool_chain"], 1)
                t.wait("pool_chain")

            def inv_sqrt(kind, cols, done):
                t.wait("st_" + kind)
                chain(gp.tensor_scalar(ve[kind][:, cols], mv[kind][:, cols, 1], EPS, 0.0, ALU.add, ALU.add))
                n = cols.stop - cols.start
                gp.tensor_tensor(rstd[kind][:, cols], ve[kind][:, cols], half[:, 0:n], ALU.pow).then_inc(done, 1)

            gp.memset(half[:], -0.5)
            gp.memset(ident[:], 0.0)
            chain(gp.memset(maskf[:], 0.0))
            gp.affine_select(out=ident[:, :], in_=ident[:, :], compare_op=ALU.not_equal, fill=1.0, base=0,
                             pattern=[[-1, P]], channel_multiplier=1)
            gp.affine_select(out=maskf[:, :], in_=maskf[:, :], compare_op=ALU.is_ge, fill=-3.0e38, base=0,
                             pattern=[[-1, P]], channel_multiplier=1).then_inc(q["pool_consts"], 1)

            gp.memset(w1s[:], 0.0)
            chain(gp.memset(w3s[:], 0.0))
            for src, sh, dst in ((w1, sw1, w1s), (w3, sw3, w3s)):
                flat = dst[:, 2:, :].rearrange("p (e c) n -> p e (c n)", e=E)
                pool.dma_start(flat[:, :, 0:HID], src.rearrange("e d h -> d e h")).then_inc(q["ld_ffn"], 16)
                pool.dma_start(dst[:, 0:2, :].rearrange("p c n -> p (c n)")[:, 0:SH], sh).then_inc(q["ld_ffn"], 16)
            w2e = w2s[:, 2:, :].rearrange("p (e c) n -> p e c n", e=E)
            for e, ch in enumerate(groups):
                src = sw2 if e == 0 else w2[e - 1]
                for c, (h0, rows) in enumerate(ch):
                    dst = w2s[0:rows, c, :] if e == 0 else w2e[0:rows, e - 1, c, :]
                    pool.dma_start(dst, src[h0:h0 + rows, :]).then_inc(q["ld_ffn"], 16)

            inv_sqrt("in", slice(0, NJ), q["rs_in"])

            def split(b, free):
                if free:
                    t.wait("parts_free")
                for m in range(3):
                    wait_mono("qf_mono", 3 * b + (m + 1))
                    chain(gp.tensor_scalar(parts[:, m, 0, :], qf[:, m, :], 1.0, 0.0, ALU.mult, ALU.add))
                    chain(gp.tensor_tensor(qf[:, m, :], qf[:, m, :], parts[:, m, 0, :], ALU.subtract))
                    chain(gp.tensor_scalar(parts[:, m, 1, :], qf[:, m, :], 1.0, 0.0, ALU.mult, ALU.add))
                    gp.tensor_tensor(parts[:, m, 2, :], qf[:, m, :], parts[:, m, 1, :],
                                     ALU.subtract).then_inc(q["parts_ready"], 1)

            split(0, False)
            t.rebase()

            def body(b, attn, prev, nxt):
                y, pb = y_base(b), p_base(b)
                for s in range(SLOTS):
                    n, i = s // G, s % G
                    tail = (attn or n < NG) and (prev or n >= NG)
                    if tail and n % NG == 2 and i == 1:
                        inv_sqrt("att", slice(0, 1), q["rs_att"])
                    if tail and n % NG == 3 and i == 0:
                        inv_sqrt("x1", slice(0, 1), q["rs_x1"])
                    if prev and s in gate_at:
                        k = gate_at[s]
                        e, c, rows = items[k]
                        pool.wait_ge(q["p_mono"], pb + (k + 1))
                        chain(gp.tensor_tensor(th[:, k % 2, :], th[:, k % 2, :], prod[:, k % 2, :], ALU.mult))
                        gp.tensor_tensor(gact[:, e % 2, c, :], th[:, k % 2, :], prod[:, k % 2, :],
                                         ALU.add).then_inc(q["g_mono"], 1)
                    if prev and s in comb_at:
                        e = comb_at[s]
                        wait_mono("y_mono", y + (y_index(attn, prev, e) + 1))
                        if e == 0:
                            t.wait("out_stored", 16)
                            gp.tensor_scalar(yacc[:, :, :], yexp[:, 0, :, :], 1.0, 0.0, ALU.mult,
                                             ALU.add).then_inc(q["acc_done"], 1)
                        else:
                            gp.tensor_tensor(yacc[:, :, :], yacc[:, :, :], yexp[:, e % 2, :, :],
                                             ALU.add).then_inc(q["acc_done"], 1)
                    if nxt and n == 6 and i == 1:
                        inv_sqrt("in", slice(0, NJ), q["rs_in"])
                    if nxt and n == 9 and i == 1:
                        split(b + 1, True)
                    if prev and s == FINAL_STATS:
                        inv_sqrt("out", slice(0, NJ), q["rs_out"])
                t.rebase()

            def y_index(attn, prev, e):
                s_e = slot_of[last_item[e]] + 2
                count = e
                for s in range(s_e + 1):
                    n, i = s // G, s % G
                    tail = (attn or n < NG) and (prev or n >= NG)
                    count += tail and (n % NG, i) in ((2, 1), (3, 3))
                return count

            bodies(pool, body)
            pool.wait_ge(q["out_stored"], 16)

        @block.scalar
        def _(act):
            t = Tally(act, [("e_free", 2)])

            act.dma_start(nlam[:, :], lam.partition_broadcast(P)).then_inc(q["ld_lam"], 16)
            act.wait_ge(q["ld_lam"], 16)
            nc.scalar.activation(nlam[:, :], nlam[:, :], ACT.Exp, scale=-1.0).then_inc(q["lam_exp"], 1)
            act.wait_ge(q["pool_consts"], 1)
            nc.scalar.copy(identb[:, :], ident[:, :])
            nc.scalar.copy(maskb[:, :], maskf[:, :]).then_inc(q["pe_setup"], 1)

            def evac(dst, src, scale=None):
                t.wait("t_full")
                f = nc.scalar.copy(dst, src) if scale is None else nc.scalar.mul(dst, src, scale)
                return f

            evac(wT[:, 0:4, :].rearrange("p a b -> p (a b)"), TB[:, :]).then_inc(q["t_evac"], 1)
            t.wait("t_full")
            nc.scalar.copy(wT[:, 4, :], TB[:, 0:P])
            nc.scalar.copy(gT[:, :], TB[:, P:P + E]).then_inc(q["t_evac"], 1)

            def evac_n1():
                evac(n1T[:, :], TB[:, :]).then_inc(q["t_evac"], 1)

            def evac_qk(m):
                evac(qf[:, m, :], TB[:, :], SCALE if m == 0 else None).then_inc(q["qf_mono"], 1)

            evac_n1()
            for m in range(3):
                evac_qk(m)
            t.rebase()

            def exps(n, i, last):
                par, N = n % 2, P * (n // NG + 1)
                f = first_fill[n] + i * len(fills(n))
                for mats in fills(n):
                    t.wait("nm_ready")
                    for c, m in enumerate(mats):
                        ins = nc.scalar.activation(ex[:, par, m, i, 0:N], S[f % RING][:, c * N:(c + 1) * N],
                                                   ACT.Exp, bias=nm[:, par, i, m:m + 1], scale=1.0,
                                                   accum_out=Z[:, par, m, i:i + 1])
                    ins.then_inc(q["last_exps"] if last and f >= FILLS - RING else q["s_free"], 1)
                    f += 1

            def evac_x(n, i):
                N = P * (n // NG + 1)
                evac(xT[:, i, 0:N], TB[:, 0:N]).then_inc(q["t_evac"], 1)

            def body(b, attn, prev, nxt):
                gb = p_base(b)
                for s in range(SLOTS):
                    n, i = s // G, s % G
                    if attn and i == 0:
                        t.wait("e_free")
                    if attn:
                        exps(n, i, not nxt)
                    haveB = attn if n >= 1 else prev
                    haveC = attn if n >= 2 else prev
                    tail = (attn or n < NG) and (prev or n >= NG)
                    if tail and n % NG == 2 and i == 0:
                        evac(onT[:, :], TB[:, 0:P]).then_inc(q["t_evac"], 1)
                    if tail and n % NG == 3 and i == 2:
                        jt = (n // NG - 1) % NJ
                        evac(n2T_new[:, jt * P:(jt + 1) * P], TB[:, 0:P]).then_inc(q["t_evac"], 1)
                    if nxt and n == 7 and i == 2:
                        evac_n1()
                    if nxt and (n, i) in ((8, 0), (8, 1), (9, 0)):
                        evac_qk(((8, 0), (8, 1), (9, 0)).index((n, i)))
                    if haveC and i == 1 and n % NG == 1:
                        t.wait("o_full")
                        nc.scalar.copy(osb[:, :, :].rearrange("p a b -> p (a b)"), OB[:, :]).then_inc(q["o_evac"], 1)
                    if prev and s in item_at:
                        k = item_at[s]
                        if k >= 2:
                            act.wait_ge(q["g_mono"], gb + (k - 1))
                        t.wait("h1_full")
                        nc.scalar.activation(th[:, k % 2, :], H1B[:, :], ACT.Tanh, scale=0.5)
                        nc.scalar.mul(prod[:, k % 2, :], H1B[:, :], 0.5).then_inc(q["h1c_ready"], 1)
                    nb = (n - 1) % STEPS
                    if haveB and i >= 2:
                        evac_x(nb, 2 * (i - 2))
                        evac_x(nb, 2 * (i - 2) + 1)
                    if attn and n == 1 and i == 3:
                        t.wait("t_full")
                        nc.scalar.copy(vpad[:, :, :, 0:HD].rearrange("p a b c -> p (a b) c"),
                                       TB[:, :].rearrange("p (a c) -> p a c", c=HD)).then_inc(q["t_evac"], 1)
                    if prev and s == NG * G + 1:
                        t.wait("logits_ready")
                        nc.scalar.activation(sc[:, :, :].rearrange("p a b -> p (a b)"),
                                             lg[:, :, :].rearrange("p a b -> p (a b)"),
                                             ACT.Exp).then_inc(q["gexp_ready"], 1)
                t.rebase()

            bodies(act, body)

        @block.vector
        def _(dve):
            t = Tally(dve)
            v = nc.vector

            def chain(ins):
                ins.then_inc(q["dve_chain"], 1)
                t.wait("dve_chain")

            def note(ins):
                ins.then_inc(q["dve_chain"], 1)
                return t.next("dve_chain")

            def after(mark):
                dve.wait_ge(q["dve_chain"], mark)

            def stats(kind, src, cols):
                for c, a in zip(cols, src):
                    m = note(v.bn_stats(bst[kind][:, c, :], a))
                after(m)
                for c in cols:
                    ins = v.bn_aggr(mv[kind][:, c, :], bst[kind][:, c, :])
                ins.then_inc(q["st_" + kind], 1)

            def normalise(dst, src, kind, c):
                return v.tensor_scalar(dst, src, mv[kind][:, c, 0:1], rstd[kind][:, c:c + 1],
                                       ALU.subtract, ALU.mult)

            v.memset(vpad[:], 0.0)
            chain(v.memset(keep[:], 1.0))
            chain(v.memset(keep[:, :, 0:1], 0.0))

            def fence():
                chain(v.memset(fence_cell[:, :], 0.0))

            def ln_in_stats():
                t.wait("ld_x", 16)
                stats("in", [xin[:, j, :] for j in range(NJ)], range(NJ))

            def ln_in_apply():
                t.wait("rs_in")
                for j in range(NJ):
                    ins = normalise(xin[:, j, :], xin[:, j, :], "in", j)
                ins.then_inc(q["n1_ready"], 1)

            ln_in_stats()
            ln_in_apply()
            dve.wait_ge(q["lam_exp"], 1)
            chain(v.tensor_scalar(nlam[:, :], nlam[:, :], 1.0, None, ALU.add))
            chain(v.reciprocal(nlam[:, :], nlam[:, :]))
            chain(v.tensor_scalar(nlam[:, :], nlam[:, :], -1.0, None, ALU.mult))
            t.rebase()

            def row_max(n, i):
                par, N = n % 2, P * (n // NG + 1)
                f = first_fill[n] + i * len(fills(n))
                for mats in fills(n):
                    t.wait("s_full")
                    v.tensor_reduce(nm[:, par, i, mats[0]:mats[-1] + 1],
                                    S[f % RING][:, 0:len(mats) * N].rearrange("p (m n) -> p m n", n=N),
                                    AX.X, ALU.max, negate=True).then_inc(q["nm_ready"], 1)
                    f += 1

            def coefs(n):
                par, g = n % 2, n % NG
                chain(v.reciprocal(rz[:, :], Z[:, par, 1, :]))
                chain(v.tensor_tensor(cz[:, :], rz[:, :], Z[:, par, 0, :], ALU.mult))
                chain(v.tensor_tensor(nc_[:, :], cz[:, :], nlam[:, G * g:G * g + G], ALU.mult))

            def combine(n, i):
                par, N = n % 2, P * (n // NG + 1)
                v.scalar_tensor_tensor(out=ex[:, par, 0, i, 0:N], in0=ex[:, par, 1, i, 0:N],
                                       scalar=nc_[:, i:i + 1], in1=ex[:, par, 0, i, 0:N],
                                       op0=ALU.mult, op1=ALU.add).then_inc(q["x_ready"], 1)

            def abs_sums(n):
                par, g, N = n % 2, n % NG, P * (n // NG + 1)
                chain(v.tensor_scalar(zg[:, :], Z[:, par, 0, :], 1e-6, None, ALU.mult))
                v.tensor_reduce(sab[:, :], ex[:, par, 0, :, 0:N], AX.X, ALU.add,
                                apply_absolute_value=True).then_inc(q["e_free"], 1)

            def denominators(n):
                g = n % NG
                v.tensor_tensor(den[:, G * g:G * g + G], sab[:, :], zg[:, :], ALU.max).then_inc(q["dve_chain"], 1)
                t.next("dve_chain")

            def tail_slot(n, i):
                jt = (n // NG - 1) % NJ
                if n % NG == 1 and i == 3:
                    after(t.n["dve_chain"])
                    chain(v.reciprocal(rden[:, :], den[:, :]))
                if n % NG == 2 and i == 0:
                    t.wait("t1_full")
                    v.tensor_tensor(on[:, :, :], TB[:, :].rearrange("p (h d) -> p h d", d=32)[:, :, 0:HD],
                                    rden[:, :].unsqueeze(2).broadcast_to([P, H, HD]),
                                    ALU.mult).then_inc(q["on_ready"], 1)
                if n % NG == 2 and i == 1:
                    t.wait("y_full")
                    v.tensor_copy(ao[:, :], YB[:, 0:D]).then_inc(q["y_mono"], 1)
                    fence()
                    stats("att", [ao[:, :]], [0])
                if n % NG == 2 and i == 3:
                    t.wait("rs_att")
                    chain(normalise(ao[:, :], ao[:, :], "att", 0))
                    if jt == 0:
                        t.wait("ld_xres", 16)
                    chain(v.tensor_tensor(x1_new[:, jt, :], ao[:, :], xres[:, jt, :], ALU.add))
                    stats("x1", [x1_new[:, jt, :]], [0])
                if n % NG == 3 and i == 1:
                    t.wait("rs_x1")
                    normalise(n2[:, :], x1_new[:, jt, :], "x1", 0).then_inc(q["n2_ready"], 1)
                    if jt == NJ - 1:
                        v.memset(xres_cell[:, :], 0.0).then_inc(q["xres_free"], 1)

            def read_logits(jt):
                t.wait("y_full")
                v.tensor_copy(lg[:, jt, :], YB[:, 0:E]).then_inc(q["y_mono"], 1)

            def router_exp():
                fence()
                chain(v.tensor_reduce(lmx[:, :], lg[:, :, :], AX.X, ALU.max))
                v.tensor_tensor(lg[:, :, :], lg[:, :, :], lmx[:, :].unsqueeze(2).broadcast_to([P, NJ, E]),
                                ALU.subtract).then_inc(q["logits_ready"], 1)
                v.tensor_copy(x1[:, :, :], x1_new[:, :, :])
                v.tensor_copy(n2T[:, :], n2T_new[:, :]).then_inc(q["n2t_ready"], 1)

            def router_top2():
                t.wait("gexp_ready")
                chain(v.tensor_reduce(se[:, :], sc[:, :, :], AX.X, ALU.add))
                chain(v.reciprocal(se[:, :], se[:, :]))
                chain(v.tensor_tensor(sc[:, :, :], sc[:, :, :], se[:, :].unsqueeze(2).broadcast_to([P, NJ, E]), ALU.mult))
                for j in range(NJ):
                    m = note(v.max(m8[:, j, :], sc[:, j, :]))
                after(m)
                second = m8[:, :, 1:2].broadcast_to([P, NJ, E])
                v.tensor_tensor(gtv[:, :, :], sc[:, :, :], second, ALU.is_gt)
                v.tensor_tensor(cgt[:, :], m8[:, :, 0], m8[:, :, 1], ALU.is_gt)
                m = note(v.tensor_tensor(eqv[:, :, :], sc[:, :, :], second, ALU.is_equal))
                after(m)
                m = note(v.tensor_copy(comb[:, :, :], eqv[:, :, :]))
                after(m)
                chain(v.tensor_tensor(comb[:, :, 0], eqv[:, :, 0], cgt[:, :], ALU.add))
                flat = "p a b -> p (a b)"
                chain(v.tensor_tensor_scan(cum[:, :, :].rearrange(flat), keep[:, :, :].rearrange(flat),
                                           comb[:, :, :].rearrange(flat), 0.0, ALU.mult, ALU.add))
                chain(v.scalar_tensor_tensor(out=eqv[:, :, :].rearrange(flat), in0=cum[:, :, :].rearrange(flat),
                                             scalar=2.0, in1=eqv[:, :, :].rearrange(flat),
                                             op0=ALU.is_le, op1=ALU.mult))
                chain(v.tensor_tensor(gtv[:, :, :], gtv[:, :, :], eqv[:, :, :], ALU.add))
                chain(v.tensor_tensor(comb[:, :, :], gtv[:, :, :], sc[:, :, :], ALU.mult))

            def body(b, attn, prev, nxt):
                for s in range(SLOTS):
                    n, i = s // G, s % G
                    tail = (attn or n < NG) and (prev or n >= NG)
                    haveB = attn if n >= 1 else prev
                    nb = (n - 1) % STEPS
                    if attn:
                        row_max(n, i)
                    if n % NG == 0 and i == 0 and (prev if n <= NG else attn):
                        read_logits((n // NG - 2) % NJ)
                    if prev and s in comb_at:
                        e = comb_at[s]
                        t.wait("y_full")
                        if e >= 2:
                            dve.wait_ge(q["acc_done"], e - 1)
                        dst = yexp[:, e % 2, :, :]
                        src = YB[:, :].rearrange("p (j d) -> p j d", j=NJ)
                        if e == 0:
                            v.tensor_copy(dst, src).then_inc(q["y_mono"], 1)
                        else:
                            v.tensor_tensor(dst, src, comb[:, :, e - 1:e].broadcast_to([P, NJ, D]),
                                            ALU.mult).then_inc(q["y_mono"], 1)
                    if tail:
                        tail_slot(n, i)
                    if prev and s in gate_at:
                        k = gate_at[s]
                        t.wait("h1c_ready")
                        t.wait("h3_full")
                        v.tensor_tensor(prod[:, k % 2, :], prod[:, k % 2, :], H3B[:, :],
                                        ALU.mult).then_inc(q["p_mono"], 1)
                    if prev and s == NG * G:
                        router_exp()
                    if prev and s == NG * G + 2:
                        router_top2()
                    if haveB and i == 2:
                        if not attn:
                            t.wait("last_exps", RING)
                        coefs(nb)
                        combine(nb, 0)
                        combine(nb, 1)
                    if haveB and i == 3:
                        combine(nb, 2)
                        combine(nb, 3)
                        abs_sums(nb)
                        fence()
                        denominators(nb)
                    if nxt and n == 6 and i == 0:
                        ln_in_stats()
                    if nxt and n == 7 and i == 1:
                        ln_in_apply()
                    if prev and s == FINAL_STATS:
                        dve.wait_ge(q["acc_done"], NE)
                        t.next("acc_done", NE)
                        stats("out", [yacc[:, j, :] for j in range(NJ)], range(NJ))
                    if prev and s == FINAL_APPLY:
                        t.wait("rs_out")
                        for j in range(NJ):
                            m = note(normalise(yacc[:, j, :], yacc[:, j, :], "out", j))
                        after(m)
                        v.tensor_tensor(yacc[:, :, :], yacc[:, :, :], x1[:, :, :],
                                        ALU.add).then_inc(q["out_ready"], 1)
                t.rebase()

            bodies(dve, body)

        @block.tensor
        def _(pe):
            t = Tally(pe, [("t_evac", 1), ("s_free", RING)])
            mm, tr = nc.tensor.matmul, nc.tensor.transpose

            def t_fill_wait():
                t.wait("t_evac")

            def t_fill_keep():
                pe.wait_ge(q["t_evac"], t.n["t_evac"] + 1)

            pe.wait_ge(q["ld_w"], 6 * 16)
            pe.wait_ge(q["pe_setup"], 1)
            t_fill_wait()
            for i in range(4):
                last = tr(TB[:, i * P:(i + 1) * P], wload[:, i * P:(i + 1) * P], ident[:, :])
            last.then_inc(q["t_full"], 1)
            t_fill_wait()
            tr(TB[:, 0:P], wload[:, 4 * P:5 * P], ident[:, :])
            tr(TB[:, P:P + E], wload[0:E, 5 * P:6 * P], ident[0:E, 0:E]).then_inc(q["t_full"], 1)

            def n1_transposes():
                t_fill_wait()
                t.wait("n1_ready")
                for j in range(NJ):
                    last = tr(TB[:, j * P:(j + 1) * P], xin[:, j, :], ident[:, :])
                last.then_inc(q["t_full"], 1)

            def project(m, b, after_projection):
                if after_projection:
                    pe.wait_ge(q["qf_mono"], 3 * b + m)
                else:
                    t_fill_keep()
                half_t = T // 2
                first = mm(TB[:, 0:half_t], wT[:, m, :], n1T[:, 0:half_t], start=True, stop=True)
                if m == 0:
                    first.then_inc(q["xin_free"], 1)
                mm(TB[:, half_t:T], wT[:, m, :], n1T[:, half_t:T], start=True, stop=True).then_inc(q["t_full"], 1)

            n1_transposes()
            for m in range(3):
                project(m, 0, m > 0)
            pe.wait_ge(q["qf_mono"], 3)
            t.rebase()

            def scores(n, i, signal=None):
                j, h = n // NG, G * (n % NG) + i
                N = P * (j + 1)
                f = first_fill[n] + i * len(fills(n))
                for mats in fills(n):
                    t.wait("s_free")
                    for c, m in enumerate(mats):
                        first = mm(S[f % RING][:, c * N:(c + 1) * N], stacks[0][:, h, j * P:(j + 1) * P],
                                   stacks[1 + m][:, h, 0:N], start=True, stop=False)
                        if signal:
                            first.then_inc(q[signal], 1)
                            signal = None
                        last = mm(S[f % RING][:, (c + 1) * N - P:(c + 1) * N], identb[:, :], maskb[:, :],
                                  start=False, stop=True)
                    last.then_inc(q["s_full"], 1)
                    f += 1

            def transposes(n, i, signal=None):
                t.wait("x_ready")
                t_fill_wait()
                for c in range(n // NG + 1):
                    last = tr(TB[:, c * P:(c + 1) * P], ex[:, n % 2, 0, i, c * P:(c + 1) * P], ident[:, :])
                    if signal and c == 0:
                        last.then_inc(q[signal], 1)
                last.then_inc(q["t_full"], 1)

            def values(n):
                j, g = n // NG, n % NG
                t_fill_keep()
                for c in range(j + 1):
                    for i in range(G):
                        last = mm(OB[32 * i:32 * i + 32, g * P:(g + 1) * P], vpad[:, c, G * g + i, :],
                                  xT[:, i, c * P:(c + 1) * P], start=(c == 0), stop=(c == j))
                if g == NG - 1:
                    last.then_inc(q["o_full"], 1)

            def body(b, attn, prev, nxt):
                pb, yb = p_base(b), y_base(b)
                yn = 0

                def y_wait():
                    nonlocal yn
                    first = isinstance(b, int) and b == 0 and yn == 0
                    if not first:
                        pe.wait_ge(q["y_mono"], yb + yn)
                    yn += 1

                for s in range(SLOTS):
                    n, i = s // G, s % G
                    tail = (attn or n < NG) and (prev or n >= NG)
                    haveB = attn if n >= 1 else prev
                    haveC = attn if n >= 2 else prev
                    nb, ncs = (n - 1) % STEPS, (n - 2) % STEPS
                    jt = (n // NG - 1) % NJ
                    if attn:
                        if n < NG and i == 0:
                            t.wait(f"stack_loaded{n}", 16 * PARTS * (PARTS + 2))
                        scores(n, i, "stack_in_use" if nxt and n == NG and i == 0 else None)
                    if tail and n % NG == 2 and i == 0:
                        t.wait("on_ready")
                        t_fill_wait()
                        tr(TB[:, 0:P], on[:, :, :].rearrange("p h d -> p (h d)"), ident[:, :]).then_inc(q["t_full"], 1)
                    if tail and n % NG == 2 and i == 1:
                        y_wait()
                        t_fill_keep()
                        mm(YB[:, 0:D], onT[:, :], wT[:, 4, :], start=True, stop=True).then_inc(q["y_full"], 1)
                    if tail and n % NG == 3 and i == 2:
                        t.wait("n2_ready")
                        t_fill_wait()
                        tr(TB[:, 0:P], n2[:, :], ident[:, :]).then_inc(q["t_full"], 1)
                    if tail and n % NG == 3 and i == 3:
                        y_wait()
                        t_fill_keep()
                        mm(YB[:, 0:E], n2T_new[:, jt * P:(jt + 1) * P], gT[:, :], start=True,
                           stop=True).then_inc(q["y_full"], 1)
                    if nxt and n == 7 and i == 2:
                        n1_transposes()
                    if nxt and (n, i) in ((8, 0), (8, 1), (9, 0)):
                        m = ((8, 0), (8, 1), (9, 0)).index((n, i))
                        project(m, b + 1, m == 1)
                    if haveC and i == 1:
                        values(ncs)
                    if prev and s in item_at:
                        k = item_at[s]
                        if k == 0:
                            t.wait("n2t_ready")
                        else:
                            pe.wait_ge(q["p_mono"], pb + k)
                        mm(H1B[:, :], w1s[:, k, :], n2T[:, :], start=True, stop=True).then_inc(q["h1_full"], 1)
                        mm(H3B[:, :], w3s[:, k, :], n2T[:, :], start=True, stop=True).then_inc(q["h3_full"], 1)
                    if prev and s in down_at:
                        e = down_at[s]
                        y_wait()
                        pe.wait_ge(q["g_mono"], pb + (last_item[e] + 1))
                        for j in range(NJ):
                            for c, (_, rows) in enumerate(groups[e]):
                                k = last_item[e] - len(groups[e]) + 1 + c
                                last = mm(YB[:, j * P:(j + 1) * P], gact[0:rows, e % 2, c, j * P:(j + 1) * P],
                                          w2s[0:rows, k, :], start=(c == 0), stop=(c == len(groups[e]) - 1))
                        last.then_inc(q["y_full"], 1)
                    if haveB and i >= 2:
                        if nxt and i == 2 and n in (8, 9):
                            pe.wait_ge(q["qf_mono"], 3 * (b + 1) + (2 if n == 8 else 3))
                        transposes(nb, 2 * (i - 2), "stack_free" if nxt and n >= STEPS - NG and i == 3 else None)
                        transposes(nb, 2 * (i - 2) + 1)
                    if attn and n == 1 and i == 3:
                        t_fill_wait()
                        for j in range(NJ):
                            last = mm(TB[:, j * P:(j + 1) * P], n1T[:, j * P:(j + 1) * P], wT[:, 3, :],
                                      start=True, stop=True)
                        last.then_inc(q["t_full"], 1)
                    if haveC and n % NG == 1 and i == 3:
                        t_fill_keep()
                        t.wait("o_evac")
                        for g in range(NG):
                            last = tr(TB[:, g * P:(g + 1) * P], osb[:, g, :], ident[:, :])
                        last.then_inc(q["t1_full"], 1)
                if attn and not prev:
                    pe.wait_ge(q["ld_ffn"], 16 * (4 + NI))
                t.rebase()

            bodies(pe, body)


_INS = ['L0_attn_x', 'L0_attn_Wq', 'L0_attn_Wk1', 'L0_attn_Wk2', 'L0_attn_Wv', 'L0_attn_Wo', 'L0_attn_lambda_logit',
        'L0_ffn_gate_w', 'L0_ffn_w1', 'L0_ffn_w2', 'L0_ffn_w3', 'L0_ffn_sw1', 'L0_ffn_sw2', 'L0_ffn_sw3']
_OUT = ((8, 512, 128), 'float32')


def kernel(**inputs):
    import numpy as _np
    import concourse.bacc as _bacc
    from concourse import mybir as _mybir
    from concourse.bass_utils import run_bass_kernel_spmd as _run

    nc = _bacc.Bacc("TRN2", target_bir_lowering=False, num_devices=1)
    arrays, args = {}, []
    for name in _INS:
        a = _np.ascontiguousarray(inputs[name])
        arrays[name] = a
        args.append(nc.dram_tensor(name, a.shape, _mybir.dt.from_np(a.dtype), kind="ExternalInput").ap())
    out = nc.dram_tensor("out", _OUT[0], _mybir.dt.from_np(_np.dtype(_OUT[1])), kind="ExternalOutput").ap()
    diff_attention_moe_layer(nc, *args, out)
    r = _run(nc, [arrays], core_ids=[0])
    return r.results[0]["out"]
```

```python
import concourse.bass as bass
from concourse import mybir
from contextlib import ExitStack


def diff_attention_moe_layer(nc, x, Wq, Wk1, Wk2, Wv, Wo, lam, gate_w, w1, w2, w3, sw1, sw2, sw3, out):
    fp32, bf16 = mybir.dt.float32, mybir.dt.bfloat16
    ALU, ACT, AX = mybir.AluOpType, mybir.ActivationFunctionType, mybir.AxisListType

    B, T, D = x.shape
    P = 128
    H = lam.shape[0]
    HD = D // H
    NJ = T // P
    G = 4
    NG = H // G
    STEPS = NJ * NG
    SLOTS = STEPS * G
    E, _, HID = w1.shape
    SH = sw1.shape[1]
    SCALE = float(HD) ** -0.5
    EPS = 1e-5
    PARTS = 3
    KR = PARTS * PARTS * HD
    RING = 3

    groups = [[(0, P), (P, SH - P)]] + [[(0, P), (P, P), (2 * P, HID - 2 * P)] for _ in range(E)]
    items = [(e, c, rows) for e, ch in enumerate(groups) for c, (_, rows) in enumerate(ch)]
    NI = len(items)
    last_item = {e: k for k, (e, _, _) in enumerate(items)}
    NE = len(groups)
    FIRST_SLOT, LAST_SLOT = 16, 55
    weight = lambda s: s // (G * NG) + 1
    span = sum(weight(s) for s in range(FIRST_SLOT, LAST_SLOT))
    item_at, acc = {}, 0
    for s in range(FIRST_SLOT, LAST_SLOT + 1):
        k = len(item_at)
        if k < NI and acc * (NI - 1) >= k * span:
            item_at[s] = k
        acc += weight(s)
    assert len(item_at) == NI
    slot_of = {k: s for s, k in item_at.items()}
    gate_at = {slot_of[k] + 1: k for k in range(NI)}
    DOWN_LAG = 3
    down_at = {slot_of[last_item[e]] + DOWN_LAG: e for e in range(NE)}
    comb_at = {slot_of[last_item[e]] + DOWN_LAG + 1: e for e in range(NE)}
    V_SLOT = 7
    N1_SLOT, QK_SLOTS, SPLIT_SLOTS = 8, (9, 11, 13), (14, 19, 24)
    STATS_SLOT, APPLY_SLOT = 2, 5
    FINAL_STATS, FINAL_APPLY = 61, 63
    assert max(comb_at) < FINAL_STATS

    scratch = nc.dram_tensor("qk_parts", (3, PARTS, HD, H, T), bf16).ap()

    ctx = ExitStack()
    with ctx:
        def sb(name, shape, dt=fp32):
            return ctx.enter_context(nc.sbuf_tensor(name, shape, dt))

        def bank(name):
            return ctx.enter_context(nc.psum_tensor(name, [P, 512], fp32))

        def sem(name):
            return ctx.enter_context(nc.semaphore(name))

        stacks = [sb(n, [KR, H, T], bf16) for n in ("q_stack", "k1_stack", "k2_stack")]
        ex = sb("ex", [P, 2, 2, G, T])
        xb = sb("xb", [P, G, T])
        xT = sb("xT", [P, G, T])
        vpad = sb("vpad", [P, NJ, H, 32])
        w1s, w3s = sb("w1s", [P, NI, P]), sb("w3s", [P, NI, P])
        w2s = sb("w2s", [P, NI, P])
        gact = sb("gact", [P, 2, 3, T])
        th, prod = sb("th", [P, 2, T]), sb("prod", [P, 2, T])
        n2T_new, n2T = sb("n2T_new", [P, T]), sb("n2T", [P, T])
        x1_new, x1 = sb("x1_new", [P, NJ, D]), sb("x1", [P, NJ, D])
        yacc, yexp = sb("yacc", [P, NJ, D]), sb("yexp", [P, 2, NJ, D])
        xin, n1T, xres = sb("xin", [P, NJ, D]), sb("n1T", [P, T]), sb("xres", [P, NJ, D])
        qf = sb("qf", [P, 3, T])
        parts = sb("parts", [P, 3, PARTS, T], bf16)
        osb = sb("osb", [P, NG, P])
        on = sb("on", [P, H, HD])
        ao, n2, onT = (osb[:, i, :] for i in range(3))
        wT = sb("wT", [P, 5, P])
        gT = sb("gT", [P, E])
        ident = sb("ident", [P, P])
        identb, maskb = sb("identb", [P, P], bf16), sb("maskb", [P, P], bf16)
        maskf = sb("maskf", [P, P])
        nlam = sb("nlam", [P, H])
        nm = sb("nm", [P, 2, G, 2])
        Z = sb("Z", [P, 2, 2, G])
        rz, cz, nc_ = sb("rz", [P, G]), sb("cz", [P, G]), sb("negc", [P, G])
        zg, den, rden, sab = sb("zg", [P, 2, G]), sb("den", [P, H]), sb("rden", [P, H]), sb("sab", [P, G])
        half = sb("half", [P, 4])
        kinds = ("in", "att", "x1", "out")
        bst = {k: sb(f"bst_{k}", [P, NJ, 6]) for k in kinds}
        mv = {k: sb(f"mv_{k}", [P, NJ, 2]) for k in kinds}
        ve = {k: sb(f"ve_{k}", [P, NJ]) for k in kinds}
        rstd = {k: sb(f"rstd_{k}", [P, NJ]) for k in kinds}
        lg, sc, se = sb("lg", [P, NJ, E]), sb("sc", [P, NJ, E]), sb("se", [P, NJ])
        m8, lmx = sb("m8", [P, NJ, 8]), sb("lmx", [P, NJ])
        gtv, eqv, cum, comb = sb("gtv", [P, NJ, E]), sb("eqv", [P, NJ, E]), sb("cum", [P, NJ, E]), sb("comb", [P, NJ, E])
        cgt, keep = sb("cgt", [P, NJ]), sb("keep", [P, NJ, E])
        fence_cell, xres_cell, pool_cell = (sb(f"{n}_cell", [P, 1]) for n in ("fence", "xres", "pool"))
        wload = xT[:, 0:2, :].rearrange("p a b -> p (a b)")

        S = [bank(f"S{i}") for i in range(RING)]
        TB, OB, H1B, H3B, YB = bank("TB"), bank("OB"), bank("H1B"), bank("H3B"), bank("YB")

        names = """
        ld_w ld_ffn ld_x ld_xres ld_lam pool_consts lam_exp
        s_full s_free nm_ready last_exps x_ready t_full t_evac
        proj_full proj_evac o_full o_evac  y_full h1_full h3_full h1c_ready acc_done n2t_ready n2_ready
        st_in st_att st_x1 st_out rs_in rs_att rs_x1 rs_out n1_ready xin_free xres_free
        parts_ready parts_stored parts_free stack_in_use stack_free logits_ready gexp_ready
        out_ready out_stored dve_chain pool_chain pe_setup
        qf_mono p_mono y_mono g_mono""".split()
        q = {n: sem(n) for n in names}
        stack_loaded = [sem(f"stack_loaded{g}") for g in range(NG)]
        q.update({f"stack_loaded{g}": s for g, s in enumerate(stack_loaded)})

        class Tally:

            def __init__(self, eng, rings=()):
                self.eng, self.n = eng, {}
                for name, depth in rings:
                    self.n[name] = -depth

            def next(self, name, k=1):
                self.n[name] = self.n.get(name, 0) + k
                return self.n[name]

            def wait(self, name, k=1):
                v = self.next(name, k)
                if v > 0:
                    self.eng.wait_ge(q[name], v)

            def rebase(self):
                for name, v in self.n.items():
                    if v > 0:
                        self.eng.wait_ge(q[name], v)
                        self.eng.sem_inc(q[name], -v)
                    self.n[name] = min(v, 0)

        def p_base(b):
            return NI * (b - 1)

        Y_BODY = NE + 5 * NJ

        def y_base(b):
            return 0 if isinstance(b, int) and b == 0 else b * Y_BODY - (NE + 5 + 1)

        block = ctx.enter_context(nc.Block())

        def bodies(eng, f):
            f(0, True, False, True)
            with eng.Fori(1, B - 1) as b:
                f(b, True, True, True)
            f(B - 1, True, True, False)
            f(B, False, True, False)

        def fills(n):
            return [[0, 1]] if n // NG <= 1 else [[0], [1]]

        def x_buffer(m, attn):
            return xb if attn or m < STEPS - 1 else ex[:, m % 2, 0, :, :]

        def lagged(n, i, attn, prev):
            m, h = (n - 1, 0) if i == G - 1 else (n - 2, i + 1)
            return m % STEPS, h, attn if m >= 0 else prev

        def h_banks(k, attn):
            return (H1B, H3B) if attn or k % 2 == 0 else (S[0], S[1])

        def logits_here(n, i, attn, prev):
            return n % NG == 0 and i == 0 and (prev if n <= NG else attn)

        TAIL_FILLS = ((2, 0), (2, 1), (2, 2), (3, 3))

        FILLS = sum(G * len(fills(n)) for n in range(STEPS))
        assert FILLS % RING == 0
        first_fill = [sum(G * len(fills(m)) for m in range(n)) for n in range(STEPS)]

        @block.sync
        def _(sp):
            t = Tally(sp)

            def store_parts_and_stack(wait_free):
                for m in range(3):
                    t.wait("parts_ready")
                    for i in range(PARTS):
                        sp.dma_start(scratch[m, i].rearrange("d h t -> h d t"),
                                     parts[:, m, i, :]).then_inc(q["parts_stored"], 16)
                t.wait("parts_stored", 16 * 3 * PARTS)
                sp.sem_inc(q["parts_free"], 1)
                for g in range(NG):
                    if wait_free:
                        t.wait("stack_free")
                    hs = slice(G * g, G * (g + 1))
                    for i in range(PARTS):
                        for jj in range(PARTS):
                            r = (PARTS * i + jj) * HD
                            sp.dma_start(stacks[0][r:r + HD, hs, :],
                                         scratch[0, i, :, hs, :]).then_inc(stack_loaded[g], 16)
                        r = PARTS * i * HD
                        for m in (1, 2):
                            sp.dma_start(stacks[m][r:r + PARTS * HD, hs, :],
                                         scratch[m, :, :, hs, :].rearrange("i d h t -> (i d) h t")
                                         ).then_inc(stack_loaded[g], 16)

            def load_rows(dst, b):
                return sp.dma_start(dst[:, :, :], x[b].rearrange("(j p) d -> p j d", p=P)
                                    if isinstance(b, int) else
                                    x[bass.ds(b, 1)].rearrange("a (j p) d -> (a p) j d", p=P))

            load_rows(xin, 0).then_inc(q["ld_x"], 16)
            for i, w in enumerate((Wq, Wk1, Wk2, Wv, Wo)):
                sp.dma_start(wload[:, i * P:(i + 1) * P], w).then_inc(q["ld_w"], 16)
            sp.dma_start(wload[0:E, 5 * P:6 * P], gate_w).then_inc(q["ld_w"], 16)
            load_rows(xres, 0).then_inc(q["ld_xres"], 16)
            store_parts_and_stack(False)

            def body(b, attn, prev, nxt):
                if nxt:
                    t.wait("xin_free")
                    load_rows(xin, b + 1).then_inc(q["ld_x"], 16)
                if prev and attn:
                    t.wait("xres_free")
                    load_rows(xres, b).then_inc(q["ld_xres"], 16)
                if nxt:
                    t.wait("stack_in_use")
                    store_parts_and_stack(True)
                if prev:
                    t.wait("out_ready")
                    o = out[b - 1].rearrange("(j p) d -> p j d", p=P) if isinstance(b, int) else \
                        out[bass.ds(b - 1, 1)].rearrange("a (j p) d -> (a p) j d", p=P)
                    sp.dma_start(o, yacc[:, :, :]).then_inc(q["out_stored"], 16)
                t.rebase()

            t.rebase()
            bodies(sp, body)

        @block.gpsimd
        def _(pool):
            t = Tally(pool)
            gp = nc.gpsimd
            pool.sem_inc(q["out_stored"], 16)

            def chain(ins):
                ins.then_inc(q["pool_chain"], 1)
                t.wait("pool_chain")

            def wait_mono(name, value):
                pool.wait_ge(q[name], value)
                pool.sem_inc(q["pool_chain"], 1)
                t.wait("pool_chain")

            def inv_sqrt(kind, cols, done):
                t.wait("st_" + kind)
                chain(gp.tensor_scalar(ve[kind][:, cols], mv[kind][:, cols, 1], EPS, 0.0, ALU.add, ALU.add))
                n = cols.stop - cols.start
                gp.tensor_tensor(rstd[kind][:, cols], ve[kind][:, cols], half[:, 0:n], ALU.pow).then_inc(done, 1)

            gp.memset(half[:], -0.5)
            gp.memset(ident[:], 0.0)
            chain(gp.memset(maskf[:], 0.0))
            gp.affine_select(out=ident[:, :], in_=ident[:, :], compare_op=ALU.not_equal, fill=1.0, base=0,
                             pattern=[[-1, P]], channel_multiplier=1)
            gp.affine_select(out=maskf[:, :], in_=maskf[:, :], compare_op=ALU.is_ge, fill=-3.0e38, base=0,
                             pattern=[[-1, P]], channel_multiplier=1).then_inc(q["pool_consts"], 1)

            gp.memset(w1s[:], 0.0)
            chain(gp.memset(w3s[:], 0.0))
            for src, sh, dst in ((w1, sw1, w1s), (w3, sw3, w3s)):
                flat = dst[:, 2:, :].rearrange("p (e c) n -> p e (c n)", e=E)
                pool.dma_start(flat[:, :, 0:HID], src.rearrange("e d h -> d e h")).then_inc(q["ld_ffn"], 16)
                pool.dma_start(dst[:, 0:2, :].rearrange("p c n -> p (c n)")[:, 0:SH], sh).then_inc(q["ld_ffn"], 16)
            w2e = w2s[:, 2:, :].rearrange("p (e c) n -> p e c n", e=E)
            for e, ch in enumerate(groups):
                src = sw2 if e == 0 else w2[e - 1]
                for c, (h0, rows) in enumerate(ch):
                    dst = w2s[0:rows, c, :] if e == 0 else w2e[0:rows, e - 1, c, :]
                    pool.dma_start(dst, src[h0:h0 + rows, :]).then_inc(q["ld_ffn"], 16)

            inv_sqrt("in", slice(0, NJ), q["rs_in"])

            def split(b, m, free):
                if free:
                    t.wait("parts_free")
                wait_mono("qf_mono", 3 * b + (m + 1))
                chain(gp.tensor_scalar(parts[:, m, 0, :], qf[:, m, :], 1.0, 0.0, ALU.mult, ALU.add))
                chain(gp.tensor_tensor(qf[:, m, :], qf[:, m, :], parts[:, m, 0, :], ALU.subtract))
                chain(gp.tensor_scalar(parts[:, m, 1, :], qf[:, m, :], 1.0, 0.0, ALU.mult, ALU.add))
                gp.tensor_tensor(parts[:, m, 2, :], qf[:, m, :], parts[:, m, 1, :],
                                 ALU.subtract).then_inc(q["parts_ready"], 1)

            for m in range(3):
                split(0, m, False)
            t.rebase()

            def body(b, attn, prev, nxt):
                y, pb = y_base(b), p_base(b)
                for s in range(SLOTS):
                    n, i = s // G, s % G
                    tail = (attn or n < NG) and (prev or n >= NG)
                    if tail and n % NG == 2 and i == 3:
                        inv_sqrt("att", slice(0, 1), q["rs_att"])
                    if tail and n % NG == 3 and i == 1:
                        inv_sqrt("x1", slice(0, 1), q["rs_x1"])
                    if prev and s in gate_at:
                        k = gate_at[s]
                        e, c, rows = items[k]
                        pool.wait_ge(q["p_mono"], pb + (k + 1))
                        chain(gp.tensor_tensor(th[:, k % 2, :], th[:, k % 2, :], prod[:, k % 2, :], ALU.mult))
                        gp.tensor_tensor(gact[:, e % 2, c, :], th[:, k % 2, :], prod[:, k % 2, :],
                                         ALU.add).then_inc(q["g_mono"], 1)
                    if prev and s in comb_at:
                        e = comb_at[s]
                        wait_mono("y_mono", y + (y_index(attn, prev, e) + 1))
                        if e == 0:
                            t.wait("out_stored", 16)
                            gp.tensor_scalar(yacc[:, :, :], yexp[:, 0, :, :], 1.0, 0.0, ALU.mult,
                                             ALU.add).then_inc(q["acc_done"], 1)
                        else:
                            chain(gp.memset(pool_cell[:, :], 0.0))
                            gp.tensor_tensor(yacc[:, :, :], yacc[:, :, :], yexp[:, e % 2, :, :],
                                             ALU.add).then_inc(q["acc_done"], 1)
                    if nxt and s == STATS_SLOT:
                        inv_sqrt("in", slice(0, NJ), q["rs_in"])
                    if nxt and s in SPLIT_SLOTS:
                        m = SPLIT_SLOTS.index(s)
                        split(b + 1, m, m == 0)
                    if prev and s == FINAL_STATS:
                        inv_sqrt("out", slice(0, NJ), q["rs_out"])
                t.rebase()

            def y_index(attn, prev, e):
                s_e = slot_of[last_item[e]] + DOWN_LAG
                count = e
                for s in range(s_e + 1):
                    n, i = s // G, s % G
                    tail = (attn or n < NG) and (prev or n >= NG)
                    count += (tail and (n % NG, i) in TAIL_FILLS) + logits_here(n, i, attn, prev)
                return count

            bodies(pool, body)
            pool.wait_ge(q["out_stored"], 16)

        @block.scalar
        def _(act):
            t = Tally(act)

            act.dma_start(nlam[:, :], lam.partition_broadcast(P)).then_inc(q["ld_lam"], 16)
            act.wait_ge(q["ld_lam"], 16)
            nc.scalar.activation(nlam[:, :], nlam[:, :], ACT.Exp, scale=-1.0).then_inc(q["lam_exp"], 1)
            act.wait_ge(q["pool_consts"], 1)
            nc.scalar.copy(identb[:, :], ident[:, :])
            nc.scalar.copy(maskb[:, :], maskf[:, :]).then_inc(q["pe_setup"], 1)

            def evac(dst, src):
                t.wait("t_full")
                return nc.scalar.copy(dst, src)

            evac(wT[:, 0:4, :].rearrange("p a b -> p (a b)"), TB[:, :]).then_inc(q["t_evac"], 1)
            t.wait("t_full")
            nc.scalar.copy(wT[:, 4, :], TB[:, 0:P])
            nc.scalar.copy(gT[:, :], TB[:, P:P + E]).then_inc(q["t_evac"], 1)

            def evac_proj(dst, src, done, scale=1.0):
                t.wait("proj_full")
                if scale == 1.0:
                    nc.scalar.copy(dst, src).then_inc(q[done], 1)
                else:
                    nc.scalar.mul(dst, src, scale).then_inc(q[done], 1)

            def evac_n1():
                evac_proj(n1T[:, :], H3B[:, :], "proj_evac")

            def evac_qk(m):
                evac_proj(qf[:, m, :], (H1B, H3B)[m % 2][:, :], "qf_mono", SCALE if m == 0 else 1.0)

            evac_n1()
            for m in range(3):
                evac_qk(m)
            t.rebase()

            def exps(n, i, last):
                par, N = n % 2, P * (n // NG + 1)
                f = first_fill[n] + i * len(fills(n))
                for mats in fills(n):
                    t.wait("nm_ready")
                    for c, m in enumerate(mats):
                        ins = nc.scalar.activation(ex[:, par, m, i, 0:N], S[f % RING][:, c * N:(c + 1) * N],
                                                   ACT.Exp, bias=nm[:, par, i, m:m + 1], scale=1.0,
                                                   accum_out=Z[:, par, m, i:i + 1])
                    ins.then_inc(q["last_exps"] if last and f >= FILLS - RING else q["s_free"], 1)
                    f += 1

            def evac_x(n, i):
                N = P * (n // NG + 1)
                evac(xT[:, i, 0:N], TB[:, 0:N]).then_inc(q["t_evac"], 1)

            def body(b, attn, prev, nxt):
                gb = p_base(b)
                for s in range(SLOTS):
                    n, i = s // G, s % G
                    if attn:
                        exps(n, i, not nxt)
                    haveC = attn if n >= 2 else prev
                    m, h, have = lagged(n, i, attn, prev)
                    if have:
                        evac_x(m, h)
                    if haveC and i == 3 and n % NG == 1:
                        t.wait("o_full")
                        nc.scalar.copy(osb[:, :, :].rearrange("p a b -> p (a b)"), OB[:, :]).then_inc(q["o_evac"], 1)
                    if attn and s == V_SLOT:
                        evac_proj(vpad[:, :, :, 0:HD].rearrange("p a b c -> p (a b) c"),
                                  H1B[:, :].rearrange("p (a c) -> p a c", c=HD), "proj_evac")
                    if nxt and s == N1_SLOT:
                        evac_n1()
                    if nxt and s in QK_SLOTS:
                        evac_qk(QK_SLOTS.index(s))
                    if prev and s in item_at:
                        k = item_at[s]
                        if k >= 2:
                            act.wait_ge(q["g_mono"], gb + (k - 1))
                        t.wait("h1_full")
                        h1_bank, _ = h_banks(k, attn)
                        nc.scalar.activation(th[:, k % 2, :], h1_bank[:, :], ACT.Tanh, scale=0.5)
                        nc.scalar.mul(prod[:, k % 2, :], h1_bank[:, :], 0.5).then_inc(q["h1c_ready"], 1)
                    if prev and s == NG * G + 1:
                        t.wait("logits_ready")
                        nc.scalar.activation(sc[:, :, :].rearrange("p a b -> p (a b)"),
                                             lg[:, :, :].rearrange("p a b -> p (a b)"),
                                             ACT.Exp).then_inc(q["gexp_ready"], 1)
                t.rebase()

            bodies(act, body)

        @block.vector
        def _(dve):
            t = Tally(dve)
            v = nc.vector

            def chain(ins):
                ins.then_inc(q["dve_chain"], 1)
                t.wait("dve_chain")

            def note(ins):
                ins.then_inc(q["dve_chain"], 1)
                return t.next("dve_chain")

            def after(mark):
                dve.wait_ge(q["dve_chain"], mark)

            def stats(kind, src, cols):
                for c, a in zip(cols, src):
                    m = note(v.bn_stats(bst[kind][:, c, :], a))
                after(m)
                for c in cols:
                    ins = v.bn_aggr(mv[kind][:, c, :], bst[kind][:, c, :])
                ins.then_inc(q["st_" + kind], 1)

            def normalise(dst, src, kind, c):
                return v.tensor_scalar(dst, src, mv[kind][:, c, 0:1], rstd[kind][:, c:c + 1],
                                       ALU.subtract, ALU.mult)

            v.memset(vpad[:], 0.0)
            chain(v.memset(keep[:], 1.0))
            chain(v.memset(keep[:, :, 0:1], 0.0))

            def fence():
                chain(v.memset(fence_cell[:, :], 0.0))

            def ln_in_stats():
                t.wait("ld_x", 16)
                stats("in", [xin[:, j, :] for j in range(NJ)], range(NJ))

            def ln_in_apply():
                t.wait("rs_in")
                for j in range(NJ):
                    ins = normalise(xin[:, j, :], xin[:, j, :], "in", j)
                ins.then_inc(q["n1_ready"], 1)

            ln_in_stats()
            ln_in_apply()
            dve.wait_ge(q["lam_exp"], 1)
            chain(v.tensor_scalar(nlam[:, :], nlam[:, :], 1.0, None, ALU.add))
            chain(v.reciprocal(nlam[:, :], nlam[:, :]))
            chain(v.tensor_scalar(nlam[:, :], nlam[:, :], -1.0, None, ALU.mult))
            t.rebase()

            def row_max(n, i):
                par, N = n % 2, P * (n // NG + 1)
                f = first_fill[n] + i * len(fills(n))
                for mats in fills(n):
                    t.wait("s_full")
                    v.tensor_reduce(nm[:, par, i, mats[0]:mats[-1] + 1],
                                    S[f % RING][:, 0:len(mats) * N].rearrange("p (m n) -> p m n", n=N),
                                    AX.X, ALU.max, negate=True).then_inc(q["nm_ready"], 1)
                    f += 1

            def coefs_and_abs_sums(n, haveB, haveC):
                m, par = (n - 1) % STEPS, (n - 1) % 2
                g = m % NG
                if haveB:
                    note(v.reciprocal(rz[:, :], Z[:, par, 1, :]))
                    note(v.tensor_scalar(zg[:, par, :], Z[:, par, 0, :], 1e-6, None, ALU.mult))
                    note(v.tensor_tensor(cz[:, :], nlam[:, G * g:G * g + G], Z[:, par, 0, :], ALU.mult))
                if haveC:
                    if not haveB:
                        note(v.memset(fence_cell[:, :], 0.0))
                    N = P * ((n - 2) % STEPS // NG + 1)
                    after(t.n["dve_chain"])
                    src = x_buffer((n - 2) % STEPS, haveB)
                    note(v.tensor_reduce(sab[:, :], src[:, :, 0:N], AX.X, ALU.add, apply_absolute_value=True))
                if haveB:
                    if not haveC:
                        after(t.n["dve_chain"])
                    mark = note(v.tensor_tensor(nc_[:, :], cz[:, :], rz[:, :], ALU.mult))
                    after(mark)

            def denominators(m):
                g = m % NG
                after(t.n["dve_chain"])
                note(v.tensor_tensor(den[:, G * g:G * g + G], sab[:, :], zg[:, m % 2, :], ALU.max))

            def combine(m, h, dst):
                par, N = m % 2, P * (m // NG + 1)
                v.scalar_tensor_tensor(out=dst[:, h, 0:N], in0=ex[:, par, 1, h, 0:N],
                                       scalar=nc_[:, h:h + 1], in1=ex[:, par, 0, h, 0:N],
                                       op0=ALU.mult, op1=ALU.add).then_inc(q["x_ready"], 1)

            def tail_slot(n, i):
                jt = (n // NG - 1) % NJ
                if n % NG == 2 and i == 0:
                    after(t.n["dve_chain"])
                    chain(v.reciprocal(rden[:, :], den[:, :]))
                    t.wait("y_full")
                    v.tensor_tensor(on[:, :, :], YB[:, :].rearrange("p (h d) -> p h d", d=32)[:, :, 0:HD],
                                    rden[:, :].unsqueeze(2).broadcast_to([P, H, HD]),
                                    ALU.mult).then_inc(q["y_mono"], 1)
                if n % NG == 2 and i == 1:
                    t.wait("y_full")
                    v.tensor_copy(onT[:, :], YB[:, 0:P]).then_inc(q["y_mono"], 1)
                if n % NG == 2 and i == 2:
                    t.wait("y_full")
                    v.tensor_copy(ao[:, :], YB[:, 0:D]).then_inc(q["y_mono"], 1)
                    fence()
                    stats("att", [ao[:, :]], [0])
                if n % NG == 3 and i == 0:
                    t.wait("rs_att")
                    chain(normalise(ao[:, :], ao[:, :], "att", 0))
                    if jt == 0:
                        t.wait("ld_xres", 16)
                    chain(v.tensor_tensor(x1_new[:, jt, :], ao[:, :], xres[:, jt, :], ALU.add))
                    stats("x1", [x1_new[:, jt, :]], [0])
                if n % NG == 3 and i == 2:
                    t.wait("rs_x1")
                    normalise(n2[:, :], x1_new[:, jt, :], "x1", 0).then_inc(q["n2_ready"], 1)
                    if jt == NJ - 1:
                        v.memset(xres_cell[:, :], 0.0).then_inc(q["xres_free"], 1)
                if n % NG == 3 and i == 3:
                    t.wait("y_full")
                    v.tensor_copy(n2T_new[:, jt * P:(jt + 1) * P], YB[:, 0:P]).then_inc(q["y_mono"], 1)
                    if jt == NJ - 1:
                        fence()
                        v.tensor_copy(n2T[:, :], n2T_new[:, :]).then_inc(q["n2t_ready"], 1)
                        v.tensor_copy(x1[:, :, :], x1_new[:, :, :])

            def read_logits(jt):
                t.wait("y_full")
                v.tensor_copy(lg[:, jt, :], YB[:, 0:E]).then_inc(q["y_mono"], 1)

            def router_exp():
                fence()
                chain(v.tensor_reduce(lmx[:, :], lg[:, :, :], AX.X, ALU.max))
                v.tensor_tensor(lg[:, :, :], lg[:, :, :], lmx[:, :].unsqueeze(2).broadcast_to([P, NJ, E]),
                                ALU.subtract).then_inc(q["logits_ready"], 1)

            def router_top2():
                t.wait("gexp_ready")
                chain(v.tensor_reduce(se[:, :], sc[:, :, :], AX.X, ALU.add))
                chain(v.reciprocal(se[:, :], se[:, :]))
                chain(v.tensor_tensor(sc[:, :, :], sc[:, :, :], se[:, :].unsqueeze(2).broadcast_to([P, NJ, E]), ALU.mult))
                for j in range(NJ):
                    m = note(v.max(m8[:, j, :], sc[:, j, :]))
                after(m)
                second = m8[:, :, 1:2].broadcast_to([P, NJ, E])
                v.tensor_tensor(gtv[:, :, :], sc[:, :, :], second, ALU.is_gt)
                v.tensor_tensor(cgt[:, :], m8[:, :, 0], m8[:, :, 1], ALU.is_gt)
                m = note(v.tensor_tensor(eqv[:, :, :], sc[:, :, :], second, ALU.is_equal))
                after(m)
                m = note(v.tensor_copy(comb[:, :, :], eqv[:, :, :]))
                after(m)
                chain(v.tensor_tensor(comb[:, :, 0], eqv[:, :, 0], cgt[:, :], ALU.add))
                flat = "p a b -> p (a b)"
                chain(v.tensor_tensor_scan(cum[:, :, :].rearrange(flat), keep[:, :, :].rearrange(flat),
                                           comb[:, :, :].rearrange(flat), 0.0, ALU.mult, ALU.add))
                chain(v.scalar_tensor_tensor(out=eqv[:, :, :].rearrange(flat), in0=cum[:, :, :].rearrange(flat),
                                             scalar=2.0, in1=eqv[:, :, :].rearrange(flat),
                                             op0=ALU.is_le, op1=ALU.mult))
                chain(v.tensor_tensor(gtv[:, :, :], gtv[:, :, :], eqv[:, :, :], ALU.add))
                chain(v.tensor_tensor(comb[:, :, :], gtv[:, :, :], sc[:, :, :], ALU.mult))

            def body(b, attn, prev, nxt):
                for s in range(SLOTS):
                    n, i = s // G, s % G
                    tail = (attn or n < NG) and (prev or n >= NG)
                    haveB, haveC = attn if n >= 1 else prev, attn if n >= 2 else prev
                    if attn:
                        row_max(n, i)
                    if i == 2:
                        if haveB and not attn:
                            t.wait("last_exps", RING)
                        coefs_and_abs_sums(n, haveB, haveC)
                    m, h, have = (n - 1, i - 2, haveB) if i >= 2 else (n - 2, i + 2, haveC)
                    if have:
                        combine(m % STEPS, h, x_buffer(m % STEPS, attn))
                    if haveC and i == 3:
                        denominators((n - 2) % STEPS)
                    if prev and s in comb_at:
                        e = comb_at[s]
                        t.wait("y_full")
                        if e >= 2:
                            dve.wait_ge(q["acc_done"], e - 1)
                        dst = yexp[:, e % 2, :, :]
                        src = YB[:, :].rearrange("p (j d) -> p j d", j=NJ)
                        if e == 0:
                            v.tensor_copy(dst, src).then_inc(q["y_mono"], 1)
                        else:
                            v.tensor_tensor(dst, src, comb[:, :, e - 1:e].broadcast_to([P, NJ, D]),
                                            ALU.mult).then_inc(q["y_mono"], 1)
                    if prev and s in gate_at:
                        k = gate_at[s]
                        t.wait("h1c_ready")
                        t.wait("h3_full")
                        v.tensor_tensor(prod[:, k % 2, :], prod[:, k % 2, :], h_banks(k, attn)[1][:, :],
                                        ALU.mult).then_inc(q["p_mono"], 1)
                    if tail:
                        tail_slot(n, i)
                    if logits_here(n, i, attn, prev):
                        read_logits((n // NG - 2) % NJ)
                    if prev and s == NG * G + 1:
                        router_exp()
                    if prev and s == NG * G + 3:
                        router_top2()
                    if nxt and s == STATS_SLOT:
                        ln_in_stats()
                    if nxt and s == APPLY_SLOT:
                        ln_in_apply()
                    if prev and s == FINAL_STATS:
                        dve.wait_ge(q["acc_done"], NE)
                        t.next("acc_done", NE)
                        stats("out", [yacc[:, j, :] for j in range(NJ)], range(NJ))
                    if prev and s == FINAL_APPLY:
                        t.wait("rs_out")
                        for j in range(NJ):
                            m = note(normalise(yacc[:, j, :], yacc[:, j, :], "out", j))
                        after(m)
                        v.tensor_tensor(yacc[:, :, :], yacc[:, :, :], x1[:, :, :],
                                        ALU.add).then_inc(q["out_ready"], 1)
                t.rebase()

            bodies(dve, body)

        @block.tensor
        def _(pe):
            t = Tally(pe, [("t_evac", 1), ("s_free", RING)])
            mm, tr = nc.tensor.matmul, nc.tensor.transpose

            def t_fill_wait():
                t.wait("t_evac")

            def t_fill_keep():
                pe.wait_ge(q["t_evac"], t.n["t_evac"] + 1)

            pe.wait_ge(q["ld_w"], 6 * 16)
            pe.wait_ge(q["pe_setup"], 1)
            t_fill_wait()
            for i in range(4):
                last = tr(TB[:, i * P:(i + 1) * P], wload[:, i * P:(i + 1) * P], ident[:, :])
            last.then_inc(q["t_full"], 1)
            t_fill_wait()
            tr(TB[:, 0:P], wload[:, 4 * P:5 * P], ident[:, :])
            tr(TB[:, P:P + E], wload[0:E, 5 * P:6 * P], ident[0:E, 0:E]).then_inc(q["t_full"], 1)

            def n1_transposes():
                t.wait("n1_ready")
                for j in range(NJ):
                    last = tr(H3B[:, j * P:(j + 1) * P], xin[:, j, :], ident[:, :])
                last.then_inc(q["proj_full"], 1)

            def project(m, b):
                bank, half_t = (H1B, H3B)[m % 2], T // 2
                if m == 2:
                    pe.wait_ge(q["qf_mono"], 3 * b + 1)
                first = mm(bank[:, 0:half_t], wT[:, m, :], n1T[:, 0:half_t], start=True, stop=True)
                if m == 0:
                    first.then_inc(q["xin_free"], 1)
                mm(bank[:, half_t:T], wT[:, m, :], n1T[:, half_t:T], start=True, stop=True).then_inc(q["proj_full"], 1)

            n1_transposes()
            t.wait("proj_evac")
            t_fill_keep()
            for m in range(3):
                project(m, 0)
            t.rebase()

            def scores(n, i, signal=None):
                j, h = n // NG, G * (n % NG) + i
                N = P * (j + 1)
                f = first_fill[n] + i * len(fills(n))
                for mats in fills(n):
                    t.wait("s_free")
                    for c, m in enumerate(mats):
                        first = mm(S[f % RING][:, c * N:(c + 1) * N], stacks[0][:, h, j * P:(j + 1) * P],
                                   stacks[1 + m][:, h, 0:N], start=True, stop=False)
                        if signal:
                            first.then_inc(q[signal], 1)
                            signal = None
                        last = mm(S[f % RING][:, (c + 1) * N - P:(c + 1) * N], identb[:, :], maskb[:, :],
                                  start=False, stop=True)
                    last.then_inc(q["s_full"], 1)
                    f += 1

            def transposes(m, h, src, signal=None):
                t.wait("x_ready")
                t_fill_wait()
                for c in range(m // NG + 1):
                    last = tr(TB[:, c * P:(c + 1) * P], src[:, h, c * P:(c + 1) * P], ident[:, :])
                    if signal and c == 0:
                        last.then_inc(q[signal], 1)
                last.then_inc(q["t_full"], 1)

            def values(n):
                j, g = n // NG, n % NG
                t_fill_keep()
                for c in range(j + 1):
                    for i in range(G):
                        last = mm(OB[32 * i:32 * i + 32, g * P:(g + 1) * P], vpad[:, c, G * g + i, :],
                                  xT[:, i, c * P:(c + 1) * P], start=(c == 0), stop=(c == j))
                if g == NG - 1:
                    last.then_inc(q["o_full"], 1)

            def body(b, attn, prev, nxt):
                pb, yb = p_base(b), y_base(b)
                yn = 0

                def y_wait():
                    nonlocal yn
                    first = isinstance(b, int) and b == 0 and yn == 0
                    if not first:
                        pe.wait_ge(q["y_mono"], yb + yn)
                    yn += 1

                for s in range(SLOTS):
                    n, i = s // G, s % G
                    tail = (attn or n < NG) and (prev or n >= NG)
                    haveC = attn if n >= 2 else prev
                    jt = (n // NG - 1) % NJ
                    if attn:
                        if n < NG and i == 0:
                            t.wait(f"stack_loaded{n}", 16 * PARTS * (PARTS + 2))
                        scores(n, i, "stack_in_use" if nxt and n == NG - 1 and i == 0 else None)
                    if tail and n % NG == 2 and i == 0:
                        y_wait()
                        t.wait("o_evac")
                        for g in range(NG):
                            last = tr(YB[:, g * P:(g + 1) * P], osb[:, g, :], ident[:, :])
                        last.then_inc(q["y_full"], 1)
                    if tail and n % NG == 2 and i == 1:
                        y_wait()
                        tr(YB[:, 0:P], on[:, :, :].rearrange("p h d -> p (h d)"), ident[:, :]).then_inc(q["y_full"], 1)
                    if tail and n % NG == 2 and i == 2:
                        y_wait()
                        mm(YB[:, 0:D], onT[:, :], wT[:, 4, :], start=True, stop=True).then_inc(q["y_full"], 1)
                    if tail and n % NG == 3 and i == 3:
                        y_wait()
                        t.wait("n2_ready")
                        tr(YB[:, 0:P], n2[:, :], ident[:, :]).then_inc(q["y_full"], 1)
                    if logits_here(n, i, attn, prev):
                        y_wait()
                        jl = (n // NG - 2) % NJ
                        mm(YB[:, 0:E], n2T_new[:, jl * P:(jl + 1) * P], gT[:, :], start=True,
                           stop=True).then_inc(q["y_full"], 1)
                    if haveC and i == 3:
                        values((n - 2) % STEPS)
                    m, h, have = lagged(n, i, attn, prev)
                    if have:
                        transposes(m, h, x_buffer(m, attn), "stack_free" if nxt and n >= STEPS - NG and i == 3 else None)
                    if attn and s == V_SLOT:
                        for j in range(NJ):
                            last = mm(H1B[:, j * P:(j + 1) * P], n1T[:, j * P:(j + 1) * P], wT[:, 3, :],
                                      start=True, stop=True)
                        last.then_inc(q["proj_full"], 1)
                    if nxt and s == N1_SLOT:
                        n1_transposes()
                    if attn and s == QK_SLOTS[0]:
                        t.wait("proj_evac", 2 if nxt else 1)
                    if nxt and s in QK_SLOTS:
                        project(QK_SLOTS.index(s), b + 1)
                    if prev and s in down_at:
                        e = down_at[s]
                        y_wait()
                        pe.wait_ge(q["g_mono"], pb + (last_item[e] + 1))
                        for j in range(NJ):
                            for c, (_, rows) in enumerate(groups[e]):
                                k = last_item[e] - len(groups[e]) + 1 + c
                                last = mm(YB[:, j * P:(j + 1) * P], gact[0:rows, e % 2, c, j * P:(j + 1) * P],
                                          w2s[0:rows, k, :], start=(c == 0), stop=(c == len(groups[e]) - 1))
                        last.then_inc(q["y_full"], 1)
                    if prev and s in item_at:
                        k = item_at[s]
                        if k == 0:
                            t.wait("n2t_ready")
                            if nxt:
                                pe.wait_ge(q["qf_mono"], 3 * (b + 1) + 3)
                        elif attn:
                            pe.wait_ge(q["p_mono"], pb + k)
                        elif k >= 2:
                            pe.wait_ge(q["p_mono"], pb + (k - 1))
                        h1_bank, h3_bank = h_banks(k, attn)
                        mm(h1_bank[:, :], w1s[:, k, :], n2T[:, :], start=True, stop=True).then_inc(q["h1_full"], 1)
                        mm(h3_bank[:, :], w3s[:, k, :], n2T[:, :], start=True, stop=True).then_inc(q["h3_full"], 1)
                if attn and not prev:
                    pe.wait_ge(q["ld_ffn"], 16 * (4 + NI))
                t.rebase()

            bodies(pe, body)


_INS = ['L0_attn_x', 'L0_attn_Wq', 'L0_attn_Wk1', 'L0_attn_Wk2', 'L0_attn_Wv', 'L0_attn_Wo', 'L0_attn_lambda_logit',
        'L0_ffn_gate_w', 'L0_ffn_w1', 'L0_ffn_w2', 'L0_ffn_w3', 'L0_ffn_sw1', 'L0_ffn_sw2', 'L0_ffn_sw3']
_OUT = ((8, 512, 128), 'float32')


def kernel(**inputs):
    import numpy as _np
    import concourse.bacc as _bacc
    from concourse import mybir as _mybir
    from concourse.bass_utils import run_bass_kernel_spmd as _run

    nc = _bacc.Bacc("TRN2", target_bir_lowering=False, num_devices=1)
    arrays, args = {}, []
    for name in _INS:
        a = _np.ascontiguousarray(inputs[name])
        arrays[name] = a
        args.append(nc.dram_tensor(name, a.shape, _mybir.dt.from_np(a.dtype), kind="ExternalInput").ap())
    out = nc.dram_tensor("out", _OUT[0], _mybir.dt.from_np(_np.dtype(_OUT[1])), kind="ExternalOutput").ap()
    diff_attention_moe_layer(nc, *args, out)
    r = _run(nc, [arrays], core_ids=[0])
    return r.results[0]["out"]
```

```python
import concourse.bass as bass
from concourse import mybir
from contextlib import ExitStack


def diff_attention_moe_layer(nc, x, Wq, Wk1, Wk2, Wv, Wo, lam, gate_w, w1, w2, w3, sw1, sw2, sw3, out):
    fp32, bf16 = mybir.dt.float32, mybir.dt.bfloat16
    ALU, ACT, AX = mybir.AluOpType, mybir.ActivationFunctionType, mybir.AxisListType

    B, T, D = x.shape
    P = 128
    H = lam.shape[0]
    HD = D // H
    NJ = T // P
    G = 4
    NG = H // G
    STEPS = NJ * NG
    SLOTS = STEPS * G
    E, _, HID = w1.shape
    SH = sw1.shape[1]
    SCALE = float(HD) ** -0.5
    EPS = 1e-5
    PARTS = 3
    KR = PARTS * PARTS * HD
    RING = 3

    groups = [[P, SH - P]] + [[P, P, HID - 2 * P] for _ in range(E)]
    chunks = [(e, c, rows) for e, ch in enumerate(groups) for c, rows in enumerate(ch)]
    NC, NI, HT = len(chunks), 2 * len(chunks), T // 2
    items = [(e, c, rows, half) for e, c, rows in chunks for half in range(2)]
    NE = len(groups)
    first_item = [min(k for k in range(NI) if items[k][0] == e) for e in range(NE)]
    last_item = [max(k for k in range(NI) if items[k][0] == e) for e in range(NE)]

    T1, T2, WO, T4, LOGITS = (2, 1), (2, 2), (2, 3), (0, 0), (0, 1)
    TAIL_FILLS = (T1, T2, WO, T4, LOGITS)

    def plan(rate):
        item_at, down_at, k, credit, waiting = {}, {}, 0, 1.0, []
        for s in range(FIRST_SLOT, SLOTS):
            n, i = s // G, s % G
            credit = min(credit + rate * (BASE + n // NG + 1), 3.0)
            if waiting and waiting[0][1] + DOWN_LAG <= s and (n % NG, i) not in TAIL_FILLS:
                down_at[s] = waiting.pop(0)[0]
                continue
            item_at[s] = []
            while k < NI and credit >= 1.0 and len(item_at[s]) < 2:
                if waiting and waiting[0][0] <= items[k][0] - 2:
                    break
                item_at[s].append(k)
                credit -= 1.0
                if k in last_item:
                    waiting.append((items[k][0], s))
                k += 1
        return item_at, down_at, k == NI and not waiting

    FIRST_SLOT, DOWN_LAG, BASE, LAST_DOWN = 17, 3, 1.0, 59
    rate = 0.05
    while not plan(rate)[2] or max(plan(rate)[1]) > LAST_DOWN:
        rate += 0.005
    item_at, down_at, _ = plan(rate)
    slot_of = {k: s for s, ks in item_at.items() for k in ks}
    down_slot = {e: s for s, e in down_at.items()}
    gate_at = {s + 1: ks for s, ks in item_at.items()}
    comb_at = {s + 1: e for s, e in down_at.items()}
    assert all(slot_of[first_item[e + 2]] > down_slot[e] for e in range(NE - 2))
    FINAL_STATS, FINAL_APPLY = 61, 63
    V_SLOT = 8
    N1_SLOT, QK_SLOTS, SPLIT_SLOTS = 9, (10, 12, 14), (15, 22, 29)
    STATS_SLOT, APPLY_SLOT = 4, 7
    scratch = nc.dram_tensor("qk_parts", (3, PARTS, HD, H, T), bf16).ap()

    ctx = ExitStack()
    with ctx:
        def sb(name, shape, dt=fp32):
            return ctx.enter_context(nc.sbuf_tensor(name, shape, dt))

        def bank(name):
            return ctx.enter_context(nc.psum_tensor(name, [P, 512], fp32))

        def sem(name):
            return ctx.enter_context(nc.semaphore(name))

        GR = 6
        stacks = [sb(n, [KR, H, T], bf16) for n in ("q_stack", "k1_stack", "k2_stack")]
        ex = sb("ex", [P, 2, 2, G, T])
        xb = sb("xb", [P, G, T])
        xT = sb("xT", [P, G, T])
        vpad = sb("vpad", [P, NJ, H, 32])
        w1s, w3s = sb("w1s", [P, NC, P]), sb("w3s", [P, NC, P])
        w2s = sb("w2s", [P, NC, P])
        gact = sb("gact", [P, 2, 3, T])
        th, prod = sb("th", [P, GR, HT]), sb("prod", [P, GR, HT])
        n2T_new, n2T = sb("n2T_new", [P, T]), sb("n2T", [P, T])
        x1_new, x1 = sb("x1_new", [P, NJ, D]), sb("x1", [P, NJ, D])
        yacc, yexp = sb("yacc", [P, NJ, D]), sb("yexp", [P, 2, NJ, D])
        xin, n1T, xres = sb("xin", [P, NJ, D]), sb("n1T", [P, T]), sb("xres", [P, NJ, D])
        qf = sb("qf", [P, 3, T])
        parts = sb("parts", [P, PARTS, T], bf16)
        osb = sb("osb", [P, NG, P])
        on = sb("on", [P, H, HD])
        ao, n2, onT = (osb[:, i, :] for i in range(3))
        wT = sb("wT", [P, 5, P])
        gT = sb("gT", [P, E])
        ident = sb("ident", [P, P])
        identb, maskb = sb("identb", [P, P], bf16), sb("maskb", [P, P], bf16)
        maskf = sb("maskf", [P, P])
        nlam = sb("nlam", [P, H])
        nm = sb("nm", [P, 2, G, 2])
        Z = sb("Z", [P, 2, 2, G])
        rz, cz, negc = sb("rz", [P, G]), sb("cz", [P, G]), sb("negc", [P, G])
        zg, den, rden, sab = sb("zg", [P, 2, G]), sb("den", [P, H]), sb("rden", [P, H]), sb("sab", [P, 2, G])
        half = sb("half", [P, 4])
        kinds = ("in", "att", "x1", "out")
        bst = {k: sb(f"bst_{k}", [P, NJ, 6]) for k in kinds}
        mv = {k: sb(f"mv_{k}", [P, NJ, 2]) for k in kinds}
        ve = {k: sb(f"ve_{k}", [P, NJ]) for k in kinds}
        rstd = {k: sb(f"rstd_{k}", [P, NJ]) for k in kinds}
        lg, sc, se = sb("lg", [P, NJ, E]), sb("sc", [P, NJ, E]), sb("se", [P, NJ])
        m8, lmx = sb("m8", [P, NJ, 8]), sb("lmx", [P, NJ])
        gtv, eqv, cum, comb = sb("gtv", [P, NJ, E]), sb("eqv", [P, NJ, E]), sb("cum", [P, NJ, E]), sb("comb", [P, NJ, E])
        cgt, keep = sb("cgt", [P, NJ]), sb("keep", [P, NJ, E])
        fence_cell, xres_cell, pool_cell = (sb(f"{n}_cell", [P, 1]) for n in ("fence", "xres", "pool"))
        x_cell = sb("x_cell", [P, G])
        wload = xT[:, 0:2, :].rearrange("p a b -> p (a b)")

        S = [bank(f"S{i}") for i in range(RING)]
        TB, OB, HA, HB, YB = bank("TB"), bank("OB"), bank("HA"), bank("HB"), bank("YB")

        names = """
        ld_w ld_ffn ld_x ld_xres ld_lam pool_consts lam_exp
        s_full s_free nm_ready last_exps x_ready t_full t_evac abs_ready
        proj_full proj_evac o_full o_evac  y_full h_full h1c_ready acc_done n2t_ready n2_ready
        st_in st_att st_x1 st_out rs_in rs_att rs_x1 rs_out n1_ready xin_free xres_free
        parts_ready parts_stored parts_free first_parts_free stack_in_use stack_free logits_ready gexp_ready
        out_ready out_stored dve_chain pool_chain pe_setup
        qf_mono p_mono y_mono g_mono""".split()
        q = {n: sem(n) for n in names}
        stack_loaded = [sem(f"stack_loaded{g}") for g in range(NG)]
        q.update({f"stack_loaded{g}": s for g, s in enumerate(stack_loaded)})

        class Tally:

            def __init__(self, eng, rings=()):
                self.eng, self.n = eng, {}
                for name, depth in rings:
                    self.n[name] = -depth

            def next(self, name, k=1):
                self.n[name] = self.n.get(name, 0) + k
                return self.n[name]

            def wait(self, name, k=1):
                v = self.next(name, k)
                if v > 0:
                    self.eng.wait_ge(q[name], v)

            def rebase(self):
                for name, v in self.n.items():
                    if v > 0:
                        self.eng.wait_ge(q[name], v)
                        self.eng.sem_inc(q[name], -v)
                    self.n[name] = min(v, 0)

        def p_base(b):
            return NI * (b - 1)

        Y_BODY = NE + 5 * NJ

        def y_base(b):
            return 0 if isinstance(b, int) and b == 0 else b * Y_BODY - (NE + 5 + 2)

        block = ctx.enter_context(nc.Block())

        def bodies(eng, f):
            f(0, True, False, True)
            with eng.Fori(1, B - 1) as b:
                f(b, True, True, True)
            f(B - 1, True, True, False)
            f(B, False, True, False)

        def fills(n):
            return [[0, 1]] if n // NG <= 1 else [[0], [1]]

        def x_buffer(m, attn):
            return xb if attn or m < STEPS - 1 else ex[:, m % 2, 0, :, :]

        H_RING = {True: 2, False: 4}

        def h_regions(k, attn):
            bank = ([HA, HB] if attn else [HA, HB, S[0], S[1]])[k % H_RING[attn]]
            return bank[:, 0:HT], bank[:, HT:T]

        def tail_block(n, i, attn, prev):
            back = 2 if n % NG == 0 else 1
            return (n // NG - back) % NJ, attn if n // NG >= back else prev

        FILLS = sum(G * len(fills(n)) for n in range(STEPS))
        assert FILLS % RING == 0
        first_fill = [sum(G * len(fills(m)) for m in range(n)) for n in range(STEPS)]

        @block.sync
        def _(sp):
            t = Tally(sp)

            def store_parts_and_stack(wait_free):
                for m in range(3):
                    t.wait("parts_ready")
                    for i in range(PARTS):
                        sp.dma_start(scratch[m, i].rearrange("d h t -> h d t"),
                                     parts[:, i, :]).then_inc(q["parts_stored"], 16)
                    t.wait("parts_stored", 16 * PARTS)
                    if wait_free or m == 2:
                        sp.sem_inc(q["parts_free"], 1)
                    else:
                        sp.sem_inc(q["first_parts_free"], 1)
                for g in range(NG):
                    if wait_free:
                        t.wait("stack_free")
                    hs = slice(G * g, G * (g + 1))
                    for i in range(PARTS):
                        r = PARTS * i * HD
                        sp.dma_start(stacks[0][r:r + PARTS * HD, hs, :],
                                     scratch[0, i, :, hs, :].unsqueeze(0).broadcast_to([PARTS, HD, G, T])
                                     ).then_inc(stack_loaded[g], 16)
                    for m in (1, 2):
                        sp.dma_start(stacks[m][:, hs, :],
                                     scratch[m, :, :, hs, :].rearrange("j d h t -> (j d) h t").unsqueeze(0)
                                     .broadcast_to([PARTS, PARTS * HD, G, T])).then_inc(stack_loaded[g], 16)

            def load_rows(dst, b):
                return sp.dma_start(dst[:, :, :], x[b].rearrange("(j p) d -> p j d", p=P)
                                    if isinstance(b, int) else
                                    x[bass.ds(b, 1)].rearrange("a (j p) d -> (a p) j d", p=P))

            load_rows(xin, 0).then_inc(q["ld_x"], 16)
            for i, w in enumerate((Wq, Wk1, Wk2, Wv, Wo)):
                sp.dma_start(wload[:, i * P:(i + 1) * P], w).then_inc(q["ld_w"], 16)
            sp.dma_start(wload[0:E, 5 * P:6 * P], gate_w).then_inc(q["ld_w"], 16)
            load_rows(xres, 0).then_inc(q["ld_xres"], 16)
            store_parts_and_stack(False)
            def load_ffn_weights():
                for src, sh, dst in ((w1, sw1, w1s), (w3, sw3, w3s)):
                    flat = dst[:, 2:, :].rearrange("p (e c) n -> p e (c n)", e=E)
                    sp.dma_start(flat[:, :, 0:HID], src.rearrange("e d h -> d e h")).then_inc(q["ld_ffn"], 16)
                    sp.dma_start(dst[:, 0:2, :].rearrange("p c n -> p (c n)")[:, 0:SH], sh).then_inc(q["ld_ffn"], 16)
                for k, (e, c, rows) in enumerate(chunks):
                    src = sw2 if e == 0 else w2[e - 1]
                    sp.dma_start(w2s[0:rows, k, :], src[c * P:c * P + rows, :]).then_inc(q["ld_ffn"], 16)

            def body(b, attn, prev, nxt):
                if nxt:
                    t.wait("xin_free")
                    load_rows(xin, b + 1).then_inc(q["ld_x"], 16)
                if not prev:
                    load_ffn_weights()
                if prev and attn:
                    t.wait("xres_free")
                    load_rows(xres, b).then_inc(q["ld_xres"], 16)
                if nxt:
                    t.wait("stack_in_use")
                    store_parts_and_stack(True)
                if prev:
                    t.wait("out_ready")
                    o = out[b - 1].rearrange("(j p) d -> p j d", p=P) if isinstance(b, int) else \
                        out[bass.ds(b - 1, 1)].rearrange("a (j p) d -> (a p) j d", p=P)
                    sp.dma_start(o, yacc[:, :, :]).then_inc(q["out_stored"], 16)
                t.rebase()

            t.rebase()
            bodies(sp, body)

        @block.gpsimd
        def _(pool):
            t = Tally(pool)
            gp = nc.gpsimd
            pool.sem_inc(q["out_stored"], 16)

            def chain(ins):
                ins.then_inc(q["pool_chain"], 1)
                t.wait("pool_chain")

            def wait_mono(name, value):
                pool.wait_ge(q[name], value)
                pool.sem_inc(q["pool_chain"], 1)
                t.wait("pool_chain")

            def inv_sqrt(kind, cols, done):
                t.wait("st_" + kind)
                chain(gp.tensor_scalar(ve[kind][:, cols], mv[kind][:, cols, 1], EPS, 0.0, ALU.add, ALU.add))
                n = cols.stop - cols.start
                gp.tensor_tensor(rstd[kind][:, cols], ve[kind][:, cols], half[:, 0:n], ALU.pow).then_inc(done, 1)

            gp.memset(half[:], -0.5)
            gp.memset(ident[:], 0.0)
            chain(gp.memset(maskf[:], 0.0))
            gp.affine_select(out=ident[:, :], in_=ident[:, :], compare_op=ALU.not_equal, fill=1.0, base=0,
                             pattern=[[-1, P]], channel_multiplier=1)
            gp.affine_select(out=maskf[:, :], in_=maskf[:, :], compare_op=ALU.is_ge, fill=-3.0e38, base=0,
                             pattern=[[-1, P]], channel_multiplier=1).then_inc(q["pool_consts"], 1)

            for dst in (w1s, w3s):
                gp.memset(dst[:, 1, SH - P:P], 0.0).then_inc(q["ld_ffn"], 1)
                gp.memset(dst[:, 4::3, HID - 2 * P:P], 0.0).then_inc(q["ld_ffn"], 1)

            inv_sqrt("in", slice(0, NJ), q["rs_in"])

            def split(b, m):
                t.wait("parts_free")
                wait_mono("qf_mono", 3 * b + (m + 1))
                chain(gp.tensor_scalar(parts[:, 0, :], qf[:, m, :], 1.0, 0.0, ALU.mult, ALU.add))
                chain(gp.tensor_tensor(qf[:, m, :], qf[:, m, :], parts[:, 0, :], ALU.subtract))
                chain(gp.tensor_scalar(parts[:, 1, :], qf[:, m, :], 1.0, 0.0, ALU.mult, ALU.add))
                gp.tensor_tensor(parts[:, 2, :], qf[:, m, :], parts[:, 1, :],
                                 ALU.subtract).then_inc(q["parts_ready"], 1)

            t.rebase()

            def body(b, attn, prev, nxt):
                y, pb = y_base(b), p_base(b)
                for s in range(SLOTS):
                    n, i = s // G, s % G
                    _, tail = tail_block(n, i, attn, prev)
                    if tail and n % NG == 2 and i == 3:
                        inv_sqrt("att", slice(0, 1), q["rs_att"])
                    if tail and n % NG == 3 and i == 2:
                        inv_sqrt("x1", slice(0, 1), q["rs_x1"])
                    for k in gate_at.get(s, ()) if prev else ():
                        e, c, _, half = items[k]
                        pool.wait_ge(q["p_mono"], pb + (k + 1))
                        chain(gp.tensor_tensor(th[:, k % GR, :], th[:, k % GR, :], prod[:, k % GR, :], ALU.mult))
                        gp.tensor_tensor(gact[:, e % 2, c, half * HT:(half + 1) * HT], th[:, k % GR, :],
                                         prod[:, k % GR, :], ALU.add).then_inc(q["g_mono"], 1)
                    if prev and s in comb_at:
                        e = comb_at[s]
                        wait_mono("y_mono", y + (y_index(attn, prev, e) + 1))
                        if e == 0:
                            t.wait("out_stored", 16)
                            gp.tensor_scalar(yacc[:, :, :], yexp[:, 0, :, :], 1.0, 0.0, ALU.mult,
                                             ALU.add).then_inc(q["acc_done"], 1)
                        else:
                            chain(gp.memset(pool_cell[:, :], 0.0))
                            gp.tensor_tensor(yacc[:, :, :], yacc[:, :, :], yexp[:, e % 2, :, :],
                                             ALU.add).then_inc(q["acc_done"], 1)
                    if nxt and s == STATS_SLOT:
                        inv_sqrt("in", slice(0, NJ), q["rs_in"])
                    if nxt and s in SPLIT_SLOTS:
                        m = SPLIT_SLOTS.index(s)
                        split(b + 1, m)
                    if prev and s == FINAL_STATS:
                        inv_sqrt("out", slice(0, NJ), q["rs_out"])
                t.rebase()

            def y_index(attn, prev, e):
                s_e = down_slot[e]
                count = e
                for s in range(s_e + 1):
                    n, i = s // G, s % G
                    count += tail_block(n, i, attn, prev)[1] and (n % NG, i) in TAIL_FILLS
                return count

            bodies(pool, body)
            pool.wait_ge(q["out_stored"], 16)

        @block.scalar
        def _(act):
            t = Tally(act)

            act.dma_start(nlam[:, :], lam.partition_broadcast(P)).then_inc(q["ld_lam"], 16)
            act.wait_ge(q["ld_lam"], 16)
            nc.scalar.activation(nlam[:, :], nlam[:, :], ACT.Exp, scale=-1.0).then_inc(q["lam_exp"], 1)
            act.wait_ge(q["pool_consts"], 1)
            nc.scalar.copy(identb[:, :], ident[:, :])
            nc.scalar.copy(maskb[:, :], maskf[:, :]).then_inc(q["pe_setup"], 1)

            def evac(dst, src):
                t.wait("t_full")
                return nc.scalar.copy(dst, src)

            evac(wT[:, 0:4, :].rearrange("p a b -> p (a b)"), TB[:, :]).then_inc(q["t_evac"], 1)
            t.wait("t_full")
            nc.scalar.copy(wT[:, 4, :], TB[:, 0:P])
            nc.scalar.copy(gT[:, :], TB[:, P:P + E]).then_inc(q["t_evac"], 1)

            def evac_proj(dst, src, done, scale=1.0):
                t.wait("proj_full")
                if scale == 1.0:
                    nc.scalar.copy(dst, src).then_inc(q[done], 1)
                else:
                    nc.scalar.mul(dst, src, scale).then_inc(q[done], 1)

            def evac_n1():
                evac_proj(n1T[:, :], HB[:, :], "proj_evac")

            def evac_qk(m):
                evac_proj(qf[:, m, :], (HA, HB)[m % 2][:, :], "qf_mono", SCALE if m == 0 else 1.0)

            evac_n1()
            for m in range(3):
                evac_qk(m)
            t.rebase()

            def exps(n, i, last):
                par, N = n % 2, P * (n // NG + 1)
                f = first_fill[n] + i * len(fills(n))
                for mats in fills(n):
                    t.wait("nm_ready")
                    for c, m in enumerate(mats):
                        ins = nc.scalar.activation(ex[:, par, m, i, 0:N], S[f % RING][:, c * N:(c + 1) * N],
                                                   ACT.Exp, bias=nm[:, par, i, m:m + 1], scale=1.0,
                                                   accum_out=Z[:, par, m, i:i + 1])
                    ins.then_inc(q["last_exps"] if last and f >= FILLS - RING else q["s_free"], 1)
                    f += 1

            def evac_x(n, i):
                N = P * (n // NG + 1)
                evac(xT[:, i, 0:N], TB[:, 0:N]).then_inc(q["t_evac"], 1)

            def body(b, attn, prev, nxt):
                gb = p_base(b)
                for s in range(SLOTS):
                    n, i = s // G, s % G
                    if attn:
                        exps(n, i, not nxt)
                    haveC = attn if n >= 2 else prev
                    if haveC:
                        m = (n - 2) % STEPS
                        evac_x(m, i)
                        if i >= G - 2:
                            x = x_buffer(m, attn)[:, i, 0:P * (m // NG + 1)]
                            nc.scalar.activation(x, x, ACT.Abs,
                                                 accum_out=sab[:, m % 2, i:i + 1]).then_inc(q["abs_ready"], 1)
                    if tail_block(n, i, attn, prev)[1] and (n % NG, i) == (2, 0):
                        t.wait("o_full")
                        nc.scalar.copy(osb[:, :, :].rearrange("p a b -> p (a b)"), OB[:, :]).then_inc(q["o_evac"], 1)
                    if attn and s == V_SLOT:
                        evac_proj(vpad[:, :, :, 0:HD].rearrange("p a b c -> p (a b) c"),
                                  HA[:, :].rearrange("p (a c) -> p a c", c=HD), "proj_evac")
                    if nxt and s == N1_SLOT:
                        evac_n1()
                    if nxt and s in QK_SLOTS:
                        evac_qk(QK_SLOTS.index(s))
                    for k in item_at.get(s, ()) if prev else ():
                        if k >= GR:
                            act.wait_ge(q["g_mono"], gb + (k - GR + 1))
                        t.wait("h_full")
                        h1, _ = h_regions(k, attn)
                        nc.scalar.activation(th[:, k % GR, :], h1, ACT.Tanh, scale=0.5)
                        nc.scalar.mul(prod[:, k % GR, :], h1, 0.5).then_inc(q["h1c_ready"], 1)
                    if prev and s == NG * G + 2:
                        t.wait("logits_ready")
                        nc.scalar.activation(sc[:, :, :].rearrange("p a b -> p (a b)"),
                                             lg[:, :, :].rearrange("p a b -> p (a b)"),
                                             ACT.Exp).then_inc(q["gexp_ready"], 1)
                t.rebase()

            bodies(act, body)

        @block.vector
        def _(dve):
            t = Tally(dve)
            v = nc.vector

            def chain(ins):
                ins.then_inc(q["dve_chain"], 1)
                t.wait("dve_chain")

            def note(ins):
                ins.then_inc(q["dve_chain"], 1)
                return t.next("dve_chain")

            def after(mark):
                dve.wait_ge(q["dve_chain"], mark)

            def stats(kind, src, cols):
                for c, a in zip(cols, src):
                    m = note(v.bn_stats(bst[kind][:, c, :], a))
                after(m)
                for c in cols:
                    ins = v.bn_aggr(mv[kind][:, c, :], bst[kind][:, c, :])
                ins.then_inc(q["st_" + kind], 1)

            def normalise(dst, src, kind, c):
                return v.tensor_scalar(dst, src, mv[kind][:, c, 0:1], rstd[kind][:, c:c + 1],
                                       ALU.subtract, ALU.mult)

            v.memset(vpad[:], 0.0)
            chain(v.memset(keep[:], 1.0))
            chain(v.memset(keep[:, :, 0:1], 0.0))

            def fence():
                chain(v.memset(fence_cell[:, :], 0.0))

            def ln_in_stats():
                t.wait("ld_x", 16)
                stats("in", [xin[:, j, :] for j in range(NJ)], range(NJ))

            def ln_in_apply():
                t.wait("rs_in")
                for j in range(NJ):
                    ins = normalise(xin[:, j, :], xin[:, j, :], "in", j)
                ins.then_inc(q["n1_ready"], 1)

            ln_in_stats()
            ln_in_apply()
            for m in range(3):
                dve.wait_ge(q["qf_mono"], m + 1)
                if m:
                    dve.wait_ge(q["first_parts_free"], m)
                chain(v.tensor_copy(parts[:, 0, :], qf[:, m, :]))
                chain(v.tensor_tensor(qf[:, m, :], qf[:, m, :], parts[:, 0, :], ALU.subtract))
                chain(v.tensor_copy(parts[:, 1, :], qf[:, m, :]))
                v.tensor_tensor(parts[:, 2, :], qf[:, m, :], parts[:, 1, :],
                                ALU.subtract).then_inc(q["parts_ready"], 1)
            dve.wait_ge(q["lam_exp"], 1)
            chain(v.tensor_scalar(nlam[:, :], nlam[:, :], 1.0, None, ALU.add))
            chain(v.reciprocal(nlam[:, :], nlam[:, :]))
            chain(v.tensor_scalar(nlam[:, :], nlam[:, :], -1.0, None, ALU.mult))
            t.rebase()

            def row_max(n, i):
                par, N = n % 2, P * (n // NG + 1)
                f = first_fill[n] + i * len(fills(n))
                for mats in fills(n):
                    t.wait("s_full")
                    v.tensor_reduce(nm[:, par, i, mats[0]:mats[-1] + 1],
                                    S[f % RING][:, 0:len(mats) * N].rearrange("p (m n) -> p m n", n=N),
                                    AX.X, ALU.max, negate=True).then_inc(q["nm_ready"], 1)
                    f += 1

            def coefs(m):
                par, g = m % 2, m % NG
                after(t.n["dve_chain"])
                note(v.reciprocal(rz[:, :], Z[:, par, 1, :]))
                note(v.tensor_tensor(cz[:, :], nlam[:, G * g:G * g + G], Z[:, par, 0, :], ALU.mult))
                mark = note(v.tensor_scalar(zg[:, par, :], Z[:, par, 0, :], 1e-6, None, ALU.mult))
                after(mark)
                mark = note(v.tensor_tensor(negc[:, :], cz[:, :], rz[:, :], ALU.mult))
                after(mark)

            def abs_sum(m, h, src):
                after(t.n["dve_chain"])
                note(v.tensor_reduce(sab[:, m % 2, h:h + 1], src[:, h, 0:P * (m // NG + 1)], AX.X, ALU.add,
                                     apply_absolute_value=True))

            def denominators(m):
                g = m % NG
                t.wait("abs_ready")
                after(t.n["dve_chain"])
                note(v.tensor_tensor(den[:, G * g:G * g + G], sab[:, m % 2, :], zg[:, m % 2, :], ALU.max))

            def combine(m, h, dst):
                par, N = m % 2, P * (m // NG + 1)
                v.scalar_tensor_tensor(out=dst[:, h, 0:N], in0=ex[:, par, 1, h, 0:N],
                                       scalar=negc[:, h:h + 1], in1=ex[:, par, 0, h, 0:N],
                                       op0=ALU.mult, op1=ALU.add).then_inc(q["x_ready"], 1)

            def tail_slot(n, i, jt):
                if n % NG == 2 and i == 0:
                    after(t.n["dve_chain"])
                    note(v.reciprocal(rden[:, :], den[:, :]))
                if (n % NG, i) == T1:
                    after(t.n["dve_chain"])
                    t.wait("y_full")
                    v.tensor_tensor(on[:, :, :], YB[:, :].rearrange("p (h d) -> p h d", d=32)[:, :, 0:HD],
                                    rden[:, :].unsqueeze(2).broadcast_to([P, H, HD]),
                                    ALU.mult).then_inc(q["y_mono"], 1)
                if (n % NG, i) == T2:
                    t.wait("y_full")
                    v.tensor_copy(onT[:, :], YB[:, 0:P]).then_inc(q["y_mono"], 1)
                if (n % NG, i) == WO:
                    t.wait("y_full")
                    v.tensor_copy(ao[:, :], YB[:, 0:D]).then_inc(q["y_mono"], 1)
                    fence()
                    stats("att", [ao[:, :]], [0])
                if n % NG == 3 and i == 1:
                    t.wait("rs_att")
                    chain(normalise(ao[:, :], ao[:, :], "att", 0))
                    if jt == 0:
                        t.wait("ld_xres", 16)
                    chain(v.tensor_tensor(x1_new[:, jt, :], ao[:, :], xres[:, jt, :], ALU.add))
                    stats("x1", [x1_new[:, jt, :]], [0])
                if n % NG == 3 and i == 3:
                    t.wait("rs_x1")
                    normalise(n2[:, :], x1_new[:, jt, :], "x1", 0).then_inc(q["n2_ready"], 1)
                    if jt == NJ - 1:
                        v.memset(xres_cell[:, :], 0.0).then_inc(q["xres_free"], 1)
                if (n % NG, i) == T4:
                    t.wait("y_full")
                    v.tensor_copy(n2T_new[:, jt * P:(jt + 1) * P], YB[:, 0:P]).then_inc(q["y_mono"], 1)
                    if jt == NJ - 1:
                        fence()
                        v.tensor_copy(n2T[:, :], n2T_new[:, :]).then_inc(q["n2t_ready"], 1)
                        v.tensor_copy(x1[:, :, :], x1_new[:, :, :])

            def read_logits(jt):
                t.wait("y_full")
                v.tensor_copy(lg[:, jt, :], YB[:, 0:E]).then_inc(q["y_mono"], 1)

            def router_exp():
                fence()
                chain(v.tensor_reduce(lmx[:, :], lg[:, :, :], AX.X, ALU.max))
                v.tensor_tensor(lg[:, :, :], lg[:, :, :], lmx[:, :].unsqueeze(2).broadcast_to([P, NJ, E]),
                                ALU.subtract).then_inc(q["logits_ready"], 1)

            def router_top2():
                t.wait("gexp_ready")
                chain(v.tensor_reduce(se[:, :], sc[:, :, :], AX.X, ALU.add))
                chain(v.reciprocal(se[:, :], se[:, :]))
                chain(v.tensor_tensor(sc[:, :, :], sc[:, :, :], se[:, :].unsqueeze(2).broadcast_to([P, NJ, E]), ALU.mult))
                for j in range(NJ):
                    m = note(v.max(m8[:, j, :], sc[:, j, :]))
                after(m)
                second = m8[:, :, 1:2].broadcast_to([P, NJ, E])
                v.tensor_tensor(gtv[:, :, :], sc[:, :, :], second, ALU.is_gt)
                v.tensor_tensor(cgt[:, :], m8[:, :, 0], m8[:, :, 1], ALU.is_gt)
                m = note(v.tensor_tensor(eqv[:, :, :], sc[:, :, :], second, ALU.is_equal))
                after(m)
                m = note(v.tensor_copy(comb[:, :, :], eqv[:, :, :]))
                after(m)
                chain(v.tensor_tensor(comb[:, :, 0], eqv[:, :, 0], cgt[:, :], ALU.add))
                flat = "p a b -> p (a b)"
                chain(v.tensor_tensor_scan(cum[:, :, :].rearrange(flat), keep[:, :, :].rearrange(flat),
                                           comb[:, :, :].rearrange(flat), 0.0, ALU.mult, ALU.add))
                chain(v.scalar_tensor_tensor(out=eqv[:, :, :].rearrange(flat), in0=cum[:, :, :].rearrange(flat),
                                             scalar=2.0, in1=eqv[:, :, :].rearrange(flat),
                                             op0=ALU.is_le, op1=ALU.mult))
                chain(v.tensor_tensor(gtv[:, :, :], gtv[:, :, :], eqv[:, :, :], ALU.add))
                chain(v.tensor_tensor(comb[:, :, :], gtv[:, :, :], sc[:, :, :], ALU.mult))

            def body(b, attn, prev, nxt):
                for s in range(SLOTS):
                    n, i = s // G, s % G
                    jt, tail = tail_block(n, i, attn, prev)
                    haveB, haveC, haveD = (attn if n >= back else prev for back in (1, 2, 3))
                    if attn:
                        row_max(n, i)
                    for k in gate_at.get(s, ()) if prev else ():
                        t.wait("h1c_ready")
                        v.tensor_tensor(prod[:, k % GR, :], prod[:, k % GR, :], h_regions(k, attn)[1],
                                        ALU.mult).then_inc(q["p_mono"], 1)
                    m, h, have = (n - 1, 0, haveB) if i == 3 else (n - 2, i + 1, haveC)
                    if have and h < G - 2:
                        abs_sum(m % STEPS, h, x_buffer(m % STEPS, attn))
                    if haveB and i == 2:
                        if not attn:
                            t.wait("last_exps", RING)
                        coefs((n - 1) % STEPS)
                    if haveD and i == 0:
                        t.wait("abs_ready")
                    m, h, have = (n - 1, i - 2, haveB) if i >= 2 else (n - 2, i + 2, haveC)
                    if have:
                        combine(m % STEPS, h, x_buffer(m % STEPS, attn))
                        note(v.memset(x_cell[:, h % G:h % G + 1], 0.0))
                    if haveD and i == 0:
                        denominators((n - 3) % STEPS)
                    if prev and s in comb_at:
                        e = comb_at[s]
                        t.wait("y_full")
                        if e >= 2:
                            dve.wait_ge(q["acc_done"], e - 1)
                        dst = yexp[:, e % 2, :, :]
                        src = YB[:, :].rearrange("p (j d) -> p j d", j=NJ)
                        if e == 0:
                            v.tensor_copy(dst, src).then_inc(q["y_mono"], 1)
                        else:
                            v.tensor_tensor(dst, src, comb[:, :, e - 1:e].broadcast_to([P, NJ, D]),
                                            ALU.mult).then_inc(q["y_mono"], 1)
                    if tail:
                        tail_slot(n, i, jt)
                        if (n % NG, i) == LOGITS:
                            read_logits(jt)
                    if prev and s == NG * G + 2:
                        router_exp()
                    if prev and s == NG * G + 4:
                        router_top2()
                    if nxt and s == STATS_SLOT:
                        ln_in_stats()
                    if nxt and s == APPLY_SLOT:
                        ln_in_apply()
                    if prev and s == FINAL_STATS:
                        dve.wait_ge(q["acc_done"], NE)
                        t.next("acc_done", NE)
                        stats("out", [yacc[:, j, :] for j in range(NJ)], range(NJ))
                    if prev and s == FINAL_APPLY:
                        t.wait("rs_out")
                        for j in range(NJ):
                            m = note(normalise(yacc[:, j, :], yacc[:, j, :], "out", j))
                        after(m)
                        v.tensor_tensor(yacc[:, :, :], yacc[:, :, :], x1[:, :, :],
                                        ALU.add).then_inc(q["out_ready"], 1)
                t.rebase()

            bodies(dve, body)

        @block.tensor
        def _(pe):
            t = Tally(pe, [("t_evac", 1), ("s_free", RING)])
            mm, tr = nc.tensor.matmul, nc.tensor.transpose

            def t_fill_wait():
                t.wait("t_evac")

            def t_fill_keep():
                pe.wait_ge(q["t_evac"], t.n["t_evac"] + 1)

            pe.wait_ge(q["ld_w"], 6 * 16)
            pe.wait_ge(q["pe_setup"], 1)
            t_fill_wait()
            for i in range(4):
                last = tr(TB[:, i * P:(i + 1) * P], wload[:, i * P:(i + 1) * P], ident[:, :])
            last.then_inc(q["t_full"], 1)
            t_fill_wait()
            tr(TB[:, 0:P], wload[:, 4 * P:5 * P], ident[:, :])
            tr(TB[:, P:P + E], wload[0:E, 5 * P:6 * P], ident[0:E, 0:E]).then_inc(q["t_full"], 1)

            def n1_transposes():
                t.wait("n1_ready")
                for j in range(NJ):
                    last = tr(HB[:, j * P:(j + 1) * P], xin[:, j, :], ident[:, :])
                last.then_inc(q["proj_full"], 1)

            def project(m, b):
                bank, half_t = (HA, HB)[m % 2], T // 2
                if m == 2:
                    pe.wait_ge(q["qf_mono"], 3 * b + 1)
                first = mm(bank[:, 0:half_t], wT[:, m, :], n1T[:, 0:half_t], start=True, stop=True)
                if m == 0:
                    first.then_inc(q["xin_free"], 1)
                mm(bank[:, half_t:T], wT[:, m, :], n1T[:, half_t:T], start=True, stop=True).then_inc(q["proj_full"], 1)

            n1_transposes()
            t.wait("proj_evac")
            t_fill_keep()
            for m in range(3):
                project(m, 0)
            t.rebase()

            def scores(n, i, signal=None):
                j, h = n // NG, G * (n % NG) + i
                N = P * (j + 1)
                f = first_fill[n] + i * len(fills(n))
                for mats in fills(n):
                    t.wait("s_free")
                    for c, m in enumerate(mats):
                        first = mm(S[f % RING][:, c * N:(c + 1) * N], stacks[0][:, h, j * P:(j + 1) * P],
                                   stacks[1 + m][:, h, 0:N], start=True, stop=False)
                        if signal:
                            first.then_inc(q[signal], 1)
                            signal = None
                        last = mm(S[f % RING][:, (c + 1) * N - P:(c + 1) * N], identb[:, :], maskb[:, :],
                                  start=False, stop=True)
                    last.then_inc(q["s_full"], 1)
                    f += 1

            def transposes(m, h, src, signal=None):
                t.wait("x_ready")
                t_fill_wait()
                for c in range(m // NG + 1):
                    last = tr(TB[:, c * P:(c + 1) * P], src[:, h, c * P:(c + 1) * P], ident[:, :])
                    if signal and c == 0:
                        last.then_inc(q[signal], 1)
                last.then_inc(q["t_full"], 1)

            def values(n):
                j, g = n // NG, n % NG
                t_fill_keep()
                for c in range(j + 1):
                    for i in range(G):
                        last = mm(OB[32 * i:32 * i + 32, g * P:(g + 1) * P], vpad[:, c, G * g + i, :],
                                  xT[:, i, c * P:(c + 1) * P], start=(c == 0), stop=(c == j))
                if g == NG - 1:
                    last.then_inc(q["o_full"], 1)

            def body(b, attn, prev, nxt):
                pb, yb = p_base(b), y_base(b)
                yn = 0

                def y_wait():
                    nonlocal yn
                    first = isinstance(b, int) and b == 0 and yn == 0
                    if not first:
                        pe.wait_ge(q["y_mono"], yb + yn)
                    yn += 1

                for s in range(SLOTS):
                    n, i = s // G, s % G
                    jt, tail = tail_block(n, i, attn, prev)
                    haveC = attn if n >= 2 else prev
                    haveD = attn if n >= 3 else prev
                    if attn:
                        if n < NG and i == 0:
                            t.wait(f"stack_loaded{n}", 16 * (PARTS + 2))
                        scores(n, i, "stack_in_use" if nxt and n == NG - 1 and i == 0 else None)
                    if tail and (n % NG, i) == T1:
                        y_wait()
                        t.wait("o_evac")
                        for g in range(NG):
                            last = tr(YB[:, g * P:(g + 1) * P], osb[:, g, :], ident[:, :])
                        last.then_inc(q["y_full"], 1)
                    if tail and (n % NG, i) == T2:
                        y_wait()
                        tr(YB[:, 0:P], on[:, :, :].rearrange("p h d -> p (h d)"), ident[:, :]).then_inc(q["y_full"], 1)
                    if tail and (n % NG, i) == WO:
                        y_wait()
                        mm(YB[:, 0:D], onT[:, :], wT[:, 4, :], start=True, stop=True).then_inc(q["y_full"], 1)
                    if tail and (n % NG, i) == T4:
                        y_wait()
                        t.wait("n2_ready")
                        tr(YB[:, 0:P], n2[:, :], ident[:, :]).then_inc(q["y_full"], 1)
                    if tail and (n % NG, i) == LOGITS:
                        y_wait()
                        mm(YB[:, 0:E], n2T_new[:, jt * P:(jt + 1) * P], gT[:, :], start=True,
                           stop=True).then_inc(q["y_full"], 1)
                    if haveD and i == 0:
                        values((n - 3) % STEPS)
                    if haveC:
                        m = (n - 2) % STEPS
                        transposes(m, i, x_buffer(m, attn), "stack_free" if nxt and n >= STEPS - NG and i == 3 else None)
                    if attn and s == V_SLOT:
                        for j in range(NJ):
                            last = mm(HA[:, j * P:(j + 1) * P], n1T[:, j * P:(j + 1) * P], wT[:, 3, :],
                                      start=True, stop=True)
                        last.then_inc(q["proj_full"], 1)
                    if nxt and s == N1_SLOT:
                        n1_transposes()
                    if attn and s == QK_SLOTS[0]:
                        t.wait("proj_evac", 2 if nxt else 1)
                    if nxt and s in QK_SLOTS:
                        project(QK_SLOTS.index(s), b + 1)
                    if prev and s in down_at:
                        e = down_at[s]
                        y_wait()
                        pe.wait_ge(q["g_mono"], pb + (last_item[e] + 1))
                        for j in range(NJ):
                            for c, rows in enumerate(groups[e]):
                                last = mm(YB[:, j * P:(j + 1) * P], gact[0:rows, e % 2, c, j * P:(j + 1) * P],
                                          w2s[0:rows, first_item[e] // 2 + c, :],
                                          start=(c == 0), stop=(c == len(groups[e]) - 1))
                        last.then_inc(q["y_full"], 1)
                    for k in item_at.get(s, ()) if prev else ():
                        if k == 0:
                            t.wait("n2t_ready")
                            if nxt:
                                pe.wait_ge(q["qf_mono"], 3 * (b + 1) + 3)
                        if k >= H_RING[attn]:
                            pe.wait_ge(q["p_mono"], pb + (k + 1 - H_RING[attn]))
                        h1, h3 = h_regions(k, attn)
                        half = items[k][3]
                        n2_half = n2T[:, half * HT:(half + 1) * HT]
                        mm(h1, w1s[:, k // 2, :], n2_half, start=True, stop=True)
                        mm(h3, w3s[:, k // 2, :], n2_half, start=True, stop=True).then_inc(q["h_full"], 1)
                if attn and not prev:
                    pe.wait_ge(q["ld_ffn"], 16 * (4 + NC) + 4)
                t.rebase()

            bodies(pe, body)


_INS = ['L0_attn_x', 'L0_attn_Wq', 'L0_attn_Wk1', 'L0_attn_Wk2', 'L0_attn_Wv', 'L0_attn_Wo', 'L0_attn_lambda_logit',
        'L0_ffn_gate_w', 'L0_ffn_w1', 'L0_ffn_w2', 'L0_ffn_w3', 'L0_ffn_sw1', 'L0_ffn_sw2', 'L0_ffn_sw3']
_OUT = ((8, 512, 128), 'float32')


def kernel(**inputs):
    import numpy as _np
    import concourse.bacc as _bacc
    from concourse import mybir as _mybir
    from concourse.bass_utils import run_bass_kernel_spmd as _run

    nc = _bacc.Bacc("TRN2", target_bir_lowering=False, num_devices=1)
    arrays, args = {}, []
    for name in _INS:
        a = _np.ascontiguousarray(inputs[name])
        arrays[name] = a
        args.append(nc.dram_tensor(name, a.shape, _mybir.dt.from_np(a.dtype), kind="ExternalInput").ap())
    out = nc.dram_tensor("out", _OUT[0], _mybir.dt.from_np(_np.dtype(_OUT[1])), kind="ExternalOutput").ap()
    diff_attention_moe_layer(nc, *args, out)
    r = _run(nc, [arrays], core_ids=[0])
    return r.results[0]["out"]
```
